# Optimizing a Trainium2 kernel written in Bass

```python
import numpy as np
import jax
import jax.numpy as jnp

def _softmax(x, axis=-1):
    return jax.nn.softmax(x, axis=axis)

def _gelu(x):
    return jax.nn.gelu(x, approximate=True)

def _silu(x):
    return jax.nn.silu(x)

def _sigmoid(x):
    return jax.nn.sigmoid(x)

def _layernorm(x, axis=-1, eps=1e-05):
    m = jnp.mean(x, axis=axis, keepdims=True)
    v = jnp.var(x, axis=axis, keepdims=True)
    return (x - m) / jnp.sqrt(v + eps)

def _scatter_add(tgt, idx, src, axis=0):
    return tgt.at[idx].add(src)

def _segment_sum(src, seg, n):
    return jax.ops.segment_sum(src, seg, n)
kernel_name = 'mk_macaron_d1_jaxref_r8_c95df2'

def setup_inputs(seed: int=0):
    np.random.seed(seed)
    _w = jnp.asarray

    def _L0_attn_setup():
        import jax, jax.numpy as jnp
        import numpy as np
        D = 128
        H = 16
        HD = D // H
        EPS = 1e-06

        def _rmsnorm(x, w):
            xf = x.astype(jnp.float32)
            var = jnp.mean(xf * xf, axis=-1, keepdims=True)
            return (w * (xf * jax.lax.rsqrt(var + EPS))).astype(x.dtype)
        key = jax.random.key(seed)
        ks = jax.random.split(key, 10)
        B, N = (2, 256)
        s = 0.02
        return {'x': jax.random.normal(ks[0], (B, N, D), jnp.float32), 'Wq': jax.random.normal(ks[1], (D, D + H), jnp.float32) * s, 'bq': jnp.zeros((D + H,), jnp.float32), 'Wk': jax.random.normal(ks[2], (D, D), jnp.float32) * s, 'bk': jnp.zeros((D,), jnp.float32), 'Wv': jax.random.normal(ks[3], (D, D), jnp.float32) * s, 'bv': jnp.zeros((D,), jnp.float32), 'Wo': jax.random.normal(ks[4], (D, D), jnp.float32) * s, 'bo': jnp.zeros((D,), jnp.float32), 'qn_w': jnp.ones((HD,), jnp.float32), 'kn_w': jnp.ones((HD,), jnp.float32)}
    _L0_attn_in = _L0_attn_setup()

    def _L0_ffn_setup():
        import jax, jax.numpy as jnp
        import numpy as np
        N_EMBD = 128
        N_STATE = 512
        key = jax.random.key(seed)
        k_x, k_w1, k_b1, k_w2, k_b2 = jax.random.split(key, 5)
        x = jax.random.normal(k_x, (4, 256, N_EMBD), dtype=jnp.float32)
        w1 = jax.random.normal(k_w1, (N_EMBD, N_STATE), dtype=jnp.float32) * (1.0 / np.sqrt(N_EMBD))
        b1 = jax.random.normal(k_b1, (N_STATE,), dtype=jnp.float32) * 0.02
        w2 = jax.random.normal(k_w2, (N_STATE, N_EMBD), dtype=jnp.float32) * (1.0 / np.sqrt(N_STATE))
        b2 = jax.random.normal(k_b2, (N_EMBD,), dtype=jnp.float32) * 0.02
        return {'x': x, 'w1': w1, 'b1': b1, 'w2': w2, 'b2': b2}
    _L0_ffn_in = _L0_ffn_setup()
    _d = {'L0_attn_x': _L0_attn_in['x'], 'L0_attn_Wq': _L0_attn_in['Wq'], 'L0_attn_bq': _L0_attn_in['bq'], 'L0_attn_Wk': _L0_attn_in['Wk'], 'L0_attn_bk': _L0_attn_in['bk'], 'L0_attn_Wv': _L0_attn_in['Wv'], 'L0_attn_bv': _L0_attn_in['bv'], 'L0_attn_Wo': _L0_attn_in['Wo'], 'L0_attn_bo': _L0_attn_in['bo'], 'L0_attn_qn_w': _L0_attn_in['qn_w'], 'L0_attn_kn_w': _L0_attn_in['kn_w'], 'L0_ffn_w1': _L0_ffn_in['w1'], 'L0_ffn_b1': _L0_ffn_in['b1'], 'L0_ffn_w2': _L0_ffn_in['w2'], 'L0_ffn_b2': _L0_ffn_in['b2']}
    _x0 = _d['L0_attn_x']
    _d['L0_attn_x'] = jax.random.normal(jax.random.fold_in(jax.random.key(seed), 1), (2, 1024, 128), dtype=_x0.dtype)
    del _x0
    return _d

def reference(L0_attn_x, L0_attn_Wq, L0_attn_bq, L0_attn_Wk, L0_attn_bk, L0_attn_Wv, L0_attn_bv, L0_attn_Wo, L0_attn_bo, L0_attn_qn_w, L0_attn_kn_w, L0_ffn_w1, L0_ffn_b1, L0_ffn_w2, L0_ffn_b2):

    def _L0_attn_ref(x, Wq, bq, Wk, bk, Wv, bv, Wo, bo, qn_w, kn_w):
        import jax, jax.numpy as jnp
        import numpy as np
        D = 128
        H = 16
        HD = D // H
        EPS = 1e-06

        def _rmsnorm(x, w):
            xf = x.astype(jnp.float32)
            var = jnp.mean(xf * xf, axis=-1, keepdims=True)
            return (w * (xf * jax.lax.rsqrt(var + EPS))).astype(x.dtype)
        B, N, _ = x.shape
        qg = x @ Wq + bq
        Q, gate = (qg[..., :D], qg[..., D:])
        K = x @ Wk + bk
        V = x @ Wv + bv
        Q = Q.reshape(B, N, H, HD).transpose(0, 2, 1, 3)
        K = K.reshape(B, N, H, HD).transpose(0, 2, 1, 3)
        V = V.reshape(B, N, H, HD).transpose(0, 2, 1, 3)
        Q = _rmsnorm(Q, qn_w)
        K = _rmsnorm(K, kn_w)
        scores = jnp.einsum('bhqd,bhkd->bhqk', Q, K) / jnp.sqrt(jnp.float32(HD))
        attn = jax.nn.softmax(scores.astype(jnp.float32), axis=-1).astype(Q.dtype)
        out = jnp.einsum('bhqk,bhkd->bhqd', attn, V)
        out = out.transpose(0, 2, 1, 3)
        out = out * jax.nn.sigmoid(gate)[..., None]
        out = out.reshape(B, N, D)
        return out @ Wo + bo

    def _L0_ffn_ref(x, w1, b1, w2, b2):
        import jax, jax.numpy as jnp
        import numpy as np
        N_EMBD = 128
        N_STATE = 512
        h = jax.nn.gelu(jnp.einsum('bse,eh->bsh', x, w1) + b1, approximate=False)
        return jnp.einsum('bsh,he->bse', h, w2) + b2
    x = L0_attn_x
    x = x + 0.5 * _L0_ffn_ref(_layernorm(x, axis=-1), L0_ffn_w1, L0_ffn_b1, L0_ffn_w2, L0_ffn_b2)
    x = x + _L0_attn_ref(_layernorm(x, axis=-1), L0_attn_Wq, L0_attn_bq, L0_attn_Wk, L0_attn_bk, L0_attn_Wv, L0_attn_bv, L0_attn_Wo, L0_attn_bo, L0_attn_qn_w, L0_attn_kn_w)
    x = x + 0.5 * _L0_ffn_ref(_layernorm(x, axis=-1), L0_ffn_w1, L0_ffn_b1, L0_ffn_w2, L0_ffn_b2)
    return x

_drawn_inputs = setup_inputs


def setup_inputs(seed=0):
    import zlib

    import numpy as np

    out = dict(_drawn_inputs(seed))
    spreads = {'L0_attn_bq': (0.0, 0.8),
     'L0_attn_bk': (0.0, 0.8),
     'L0_attn_bv': (0.0, 0.8),
     'L0_attn_bo': (0.0, 0.1),
     'L0_attn_qn_w': (1.0, 0.6),
     'L0_attn_kn_w': (1.0, 0.6)}
    factors = {'L0_attn_Wq': 8.0,
     'L0_attn_Wk': 8.0,
     'L0_attn_Wv': 8.0,
     'L0_attn_Wo': 5.772,
     'L0_ffn_b1': 5.068,
     'L0_ffn_b2': 3.329}
    for name, (base, spread) in spreads.items():
        noise = np.random.default_rng([zlib.crc32(name.encode()), seed]).standard_normal(out[name].shape)
        drawn = base * np.exp(spread * noise) if base else spread * noise
        out[name] = jnp.asarray(drawn.astype(out[name].dtype))
    for name, factor in factors.items():
        out[name] = (out[name] * factor).astype(out[name].dtype)
    return out
```

```python
from contextlib import ExitStack

import numpy as np

import concourse.bass as bass
from concourse import mybir

F32 = mybir.dt.float32
BF16 = mybir.dt.bfloat16
I32 = mybir.dt.int32
U32 = mybir.dt.uint32
ALU = mybir.AluOpType
ACT = mybir.ActivationFunctionType
AX_X = mybir.AxisListType.X

LN_EPS = 1e-5
RMS_EPS = 1e-6
SHIFT_SAFE = 30.0


def macaron_kernel(nc, x, Wq, bq, Wk, bk, Wv, bv, Wo, bo, qn_w, kn_w, w1, b1, w2, b2, out):
    P = 128
    B, N, D = x.shape
    H = Wq.shape[1] - D
    HD = D // H
    F = w1.shape[1]
    T = B * N // P
    C = B * N // 512
    TC = T // C
    M = F // P
    assert (P, D, HD, TC, T, M) == (128, 128, 8, 4, 16, 4)
    HG = 4
    G = B * H // HG
    GB = G // B
    KT = N // P
    VW = HD + 1
    PAIRS = G // 2
    PROD = 9 * HD
    SH = 96
    ROWS = SH + 6
    STEPS = 2 * KT
    TILES = 2 * STEPS
    BT = 2 * TILES
    SBUF_OF = [0, 1, 2] * ((BT - 4) // 3) + [0, 1, 0, 2]
    PREV = [max([m for m in range(-BT, n) if SBUF_OF[m % BT] == SBUF_OF[n]]) for n in range(BT)]
    FREE3 = 3
    FREE2 = 2
    PB = 8
    ACC = 6
    LOADS = 13

    with ExitStack() as ctx:
        def sb(name, shape, dt=F32):
            return ctx.enter_context(nc.sbuf_tensor(name, shape, dt))

        def sem(name):
            return ctx.enter_context(nc.semaphore(name))

        ps = ctx.enter_context(nc.psum_tensor("ps", [P, 8, 512], F32))

        w1_sb = sb("w1_sb", [P, F])
        w2_sb = sb("w2_sb", [P, M, D])
        wq_sb = sb("wq_sb", [P, D + H])
        wk_sb = sb("wk_sb", [P, D])
        wv_sb = sb("wv_sb", [P, D])
        wo_sb = sb("wo_sb", [P, D])
        vec_rows = sb("vec_rows", [M + 4, P])
        vec_cols = sb("vec_cols", [P, M + 4])
        b1_col = vec_cols[:, 0:M]
        bq_col, bk_col, qn_col, kn_col = (vec_cols[:, M + n:M + n + 1] for n in range(4))
        qs_col = sb("qs_col", [P, 1])
        b2_row = sb("b2_row", [P, D])
        b2h_row = sb("b2h_row", [P, D])
        bo_row = sb("bo_row", [P, D])
        bv_row = sb("bv_row", [P, D])
        bg_row = sb("bg_row", [P, H])
        qn_row = sb("qn_row", [P, HD])
        kn_row = sb("kn_row", [P, HD])
        ident = sb("ident", [P, P])
        head_mean = sb("head_mean", [P, P])
        eps = sb("eps", [P, 2])
        x_in = sb("x_in", [P, T, D])
        x_b = sb("x_b", [P, T, D])
        x_1 = sb("x_1", [P, T, D])
        x_2 = sb("x_2", [P, T, D])
        y_out = x_in
        x_n = sb("x_n", [P, T, D])
        stats = sb("stats", [P, T, 6])
        mean_var = sb("mean_var", [P, T, 2])
        ln_var = sb("ln_var", [P, T])
        rstd = sb("rstd", [P, T])
        x_nT = sb("x_nT", [P, T * P])
        oT = x_nT
        qk_sum = sb("qk_sum", [P, 2, 512])
        qk_sq = sb("qk_sq", [P, 2, 512])
        qk_ln = sb("qk_ln", [P, 2, 512])
        qk_r = sb("qk_r", [P, 2, 512])
        qk_n = sb("qk_n", [P, 2, 512])
        qk_rest = sb("qk_rest", [P, 2, 512])
        parts = sb("parts", [P, 2, 3, T * P], BF16)
        v_aug = sb("v_aug", [P, G, KT, HG * VW])
        gate = sb("gate", [P, T, H])
        sig = sb("sig", [P, G, KT, HG])
        r_w = sb("r_w", [P, 4, HD])
        r_col = sb("r_col", [P, 8])
        r_bf = sb("r_bf", [P, 2], BF16)
        r_rows = sb("r_rows", [P, 3, N], BF16)
        flag = sb("flag", [P, 1], I32)
        q_st = [sb(f"q_st{p}", [P, HG, N], BF16) for p in range(2)]
        k_st = [sb(f"k_st{p}", [P, HG, N], BF16) for p in range(2)]
        v_st = [sb(f"v_st{p}", [P, KT, HG * VW]) for p in range(2)]
        probs = sb("probs", [P, PB, 1024])
        hT = probs[:, 0:4, :].rearrange("p (c m) (h n) -> p c (m h) n", c=2, h=2)
        acc_sb = sb("acc_sb", [P, 2, 512])
        r_den = sb("r_den", [P, 4, HG])
        fac = sb("fac", [P, 4, HG])
        o_nat = sb("o_nat", [P, T, D])
        mx = sb("mx", [P, HG * KT])
        mx_n = sb("mx_n", [HG * KT, P])
        mx_r = sb("mx_r", [HG * KT, P])
        mx_parts = sb("mx_parts", [HG * KT, 3, P], BF16)
        m_zero = sb("m_zero", [P, N], BF16)

        part_dram = [nc.dram_tensor(f"part_dram{s}", [B, H, 3, HD, N], BF16, kind="Internal").ap() for s in range(2)]
        m_dram = nc.dram_tensor("m_dram", [G, 3, HG * N], BF16, kind="Internal").ap()

        x_loaded = [sem(f"x_loaded{c}") for c in range(C)]
        w1_loaded = sem("w1_loaded")
        w2_loaded = sem("w2_loaded")
        vec_loaded = sem("vec_loaded")
        vec_psum = sem("vec_psum")
        vec_ready = sem("vec_ready")
        attn_w_loaded = sem("attn_w_loaded")
        rows_loaded = sem("rows_loaded")
        r_w_loaded = sem("r_w_loaded")
        wo_loaded = sem("wo_loaded")
        const_step = sem("const_step")
        consts_ready = sem("consts_ready")
        xb_ready = sem("xb_ready")
        xb2_ready = sem("xb2_ready")
        xb3_ready = sem("xb3_ready")
        stats_ready = [sem(f"stats_ready{k}") for k in range(3)]
        rstd_ready = [sem(f"rstd_ready{k}") for k in range(3)]
        xn_ready = [sem(f"xn_ready{k}") for k in range(3)]
        xnT_psum = [sem(f"xnT_psum{k}") for k in range(3)]
        xnT_ready = [sem(f"xnT_ready{k}") for k in range(3)]
        h_psum = [sem(f"h_psum{k}") for k in range(2)]
        h_ready = [sem(f"h_ready{k}") for k in range(2)]
        y_psum = [sem(f"y_psum{k}") for k in range(2)]
        y_used = [sem(f"y_used{k}") for k in range(2)]
        dve_step = sem("dve_step")
        act_step = sem("act_step")
        qk_psum = sem("qk_psum")
        v_psum = sem("v_psum")
        v_used = sem("v_used")
        gate_psum = sem("gate_psum")
        gate_sum = sem("gate_sum")
        gate_exp = sem("gate_exp")
        sig_ready = sem("sig_ready")
        sq_ready = sem("sq_ready")
        sum_ready = sem("sum_ready")
        ms_psum = sem("ms_psum")
        ln_done = sem("ln_done")
        r_ready = sem("r_ready")
        norm_ready = sem("norm_ready")
        parts_ready = sem("parts_ready")
        ones_ready = sem("ones_ready")
        r_known = sem("r_known")
        r_rows_ready = sem("r_rows_ready")
        stacks_clear = sem("stacks_clear")
        parts_stored = sem("parts_stored")
        m_stored = sem("m_stored")
        shift_rows_loaded = sem("shift_rows_loaded")
        ex_loaded = sem("ex_loaded")
        ex_scores = sem("ex_scores")
        ex_max = sem("ex_max")
        ex_mT = sem("ex_mT")
        ex_step = sem("ex_step")
        ex_parts = sem("ex_parts")
        ex_stored = sem("ex_stored")
        stack_loaded = [sem(f"stack_loaded{p}") for p in range(2)]
        stack_used = [sem(f"stack_used{p}") for p in range(2)]
        v_staged = [sem(f"v_staged{p}") for p in range(2)]
        v_st_used = [sem(f"v_st_used{p}") for p in range(2)]
        scores_ready = sem("scores_ready")
        probs_ready = sem("probs_ready")
        pv_done = sem("pv_done")
        acc_copied = sem("acc_copied")
        accT_psum = sem("accT_psum")
        norm_step = sem("norm_step")
        o_ready = sem("o_ready")
        oT_psum = sem("oT_psum")
        oT_ready = sem("oT_ready")
        o_psum = sem("o_psum")
        o_used = sem("o_used")
        out_ready = sem("out_ready")
        out_stored = sem("out_stored")

        x_dram = x.rearrange("b (t p) d -> p (b t) d", p=P)
        out_dram = out.rearrange("b (t p) d -> p (b t) d", p=P)

        def chunk(c):
            return slice(c * TC, (c + 1) * TC)

        def cols(c):
            return slice(c * 512, (c + 1) * 512)

        RSTD_GROUPS = [[[0], [1], [2], [3]], [[0, 1, 2], [3]], [[0], [1, 2, 3]]]

        def rstd_group(stage, c):
            return next(n for n, g in enumerate(RSTD_GROUPS[stage]) if c in g)

        def per_head(w):
            return bass.AP(w.tensor, w.offset, [[0, 1], [0, H], [1, HD]])

        block = ctx.enter_context(nc.Block())

        @block.sync
        def _(sp):
            for c in range(C):
                sp.dma_start(x_in[:, chunk(c), :], x_dram[:, chunk(c), :]).then_inc(x_loaded[c], 16)
                if c == 0:
                    sp.dma_start(w1_sb[:], w1).then_inc(w1_loaded, 16)
                    sp.dma_start(vec_rows[0:M, :], b1.rearrange("(m p) -> m p", p=P)).then_inc(vec_loaded, 16)
                    sp.dma_start(vec_rows[M:M + 1, :], bq[0:D].unsqueeze(0)).then_inc(vec_loaded, 16)
                    sp.dma_start(vec_rows[M + 1:M + 2, :], bk.unsqueeze(0)).then_inc(vec_loaded, 16)
                    sp.dma_start(vec_rows[M + 2:M + 3, :].rearrange("o (h d) -> o h d", d=HD),
                                 per_head(qn_w)).then_inc(vec_loaded, 16)
                    sp.dma_start(vec_rows[M + 3:M + 4, :].rearrange("o (h d) -> o h d", d=HD),
                                 per_head(kn_w)).then_inc(vec_loaded, 16)
            sp.dma_start(w2_sb[:], w2.rearrange("(m p) e -> p m e", p=P)).then_inc(w2_loaded, 16)

            for b in range(B):
                for s in range(2):
                    sp.wait_ge(parts_ready, 2 * (2 * b + 2))
                    for part in range(3):
                        sp.dma_start(part_dram[s][b, :, part], parts[:, s, part, b * N:(b + 1) * N]
                                     ).then_inc(parts_stored, 16)
            sp.wait_ge(stacks_clear, 1)
            sp.dma_start(m_dram.rearrange("g s (j n) -> (g s j) n", j=HG), m_zero[0:G * 3 * HG, :]).then_inc(m_stored, 16)
            sp.wait_ge(r_rows_ready, 1)
            for p in range(2):
                for j in range(HG):
                    sp.dma_start(q_st[p][SH:SH + 3, j, :], r_rows[0:1, :, :]).then_inc(shift_rows_loaded, 16)
            sp.wait_ge(parts_stored, 16 * 6 * B)
            sp.wait_ge(m_stored, 16)
            sp.wait_ge(shift_rows_loaded, 16 * 2 * HG)

            def load_group(g, p, done):
                q, k = (part_dram[s].rearrange("b (g j) s d t -> (b g) s d j t", j=HG) for s in range(2))
                for i in range(3):
                    for n in range(3):
                        rows = slice(HD * (3 * i + n), HD * (3 * i + n + 1))
                        sp.dma_start(q_st[p][rows, :, :], q[bass.ds(g, 1), i].rearrange("g d j t -> (g d) j t")
                                     ).then_inc(done, 16)
                    rows = slice(3 * HD * i, 3 * HD * (i + 1))
                    sp.dma_start(k_st[p][rows, :, :], k[bass.ds(g, 1)].rearrange("g s d j t -> (g s d) j t")
                                 ).then_inc(done, 16)
                sp.dma_start(q_st[p][SH + 3:SH + 6, :, :].rearrange("s j t -> s (j t)"),
                             m_dram[bass.ds(g, 1)].rearrange("g s n -> (g s) n")).then_inc(done, 16)

            sp.wait_ge(r_known, 1)
            large = sp.value_load(flag[0:1, 0:1], min_val=0, max_val=1)
            with sp.If(large > 0):
                sp.sem_inc(ex_stored, 16)
                with sp.Fori(0, G) as g:
                    sp.wait_ge(ex_parts, g + 1)
                    load_group(g, 0, ex_loaded)
                    sp.wait_ge(ex_parts, g + 2)
                    sp.dma_start(m_dram[bass.ds(g, 1)].rearrange("g s (u n) -> (g u) s n", u=HG * KT),
                                 mx_parts[:]).then_inc(ex_stored, 16)
                sp.wait_ge(ex_stored, 16 * (G + 1))

            with sp.Fori(0, PAIRS) as i:
                for p in range(2):
                    sp.wait_ge(stack_used[p], i + 1)
                    load_group(i * 2 + p, p, stack_loaded[p])

            for c in range(C):
                sp.wait_ge(out_ready, c + 1)
                sp.dma_start(out_dram[:, chunk(c), :], y_out[:, chunk(c), :]).then_inc(out_stored, 16)
            sp.wait_ge(out_stored, 16 * C)

        @block.gpsimd
        def _(pool):
            pool.dma_start(b2_row[:], b2.partition_broadcast(P)).then_inc(rows_loaded, 16)
            pool.dma_start(bo_row[:], bo.partition_broadcast(P)).then_inc(rows_loaded, 16)
            nc.gpsimd.memset(ident[:], 0.0).then_inc(const_step, 1)
            nc.gpsimd.memset(head_mean[:], 1.0 / HD).then_inc(const_step, 1)
            nc.gpsimd.memset(eps[:, 0:1], LN_EPS)
            nc.gpsimd.memset(eps[:, 1:2], RMS_EPS).then_inc(const_step, 1)
            pool.wait_ge(const_step, 3)
            nc.gpsimd.affine_select(out=ident[:], in_=ident[:], compare_op=ALU.not_equal, fill=1.0, base=0,
                                    pattern=[[-1, P]], channel_multiplier=1).then_inc(consts_ready, 1)
            hm = head_mean[:].rearrange("p (h d) -> p h d", d=HD)
            nc.gpsimd.affine_select(out=hm, in_=hm, compare_op=ALU.is_ge, fill=0.0, base=0,
                                    pattern=[[-HD, H], [0, HD]], channel_multiplier=1).then_inc(const_step, 1)
            pool.wait_ge(const_step, 4)
            nc.gpsimd.affine_select(out=hm, in_=hm, compare_op=ALU.is_ge, fill=0.0, base=HD - 1,
                                    pattern=[[HD, H], [0, HD]], channel_multiplier=-1).then_inc(consts_ready, 1)
            pool.wait_ge(rows_loaded, 32)
            nc.gpsimd.tensor_scalar(b2h_row[:], b2_row[:], 0.5, None, ALU.mult).then_inc(const_step, 1)
            pool.wait_ge(const_step, 5)
            for c in range(C):
                pool.wait_ge(x_loaded[c], 16)
                nc.gpsimd.tensor_tensor(x_b[:, chunk(c), :], x_in[:, chunk(c), :],
                                        b2h_row[:].unsqueeze(1).to_broadcast([P, TC, D]), ALU.add).then_inc(xb_ready, 1)
            nc.gpsimd.memset(v_aug[:], 1.0).then_inc(ones_ready, 1)
            for p in range(2):
                nc.gpsimd.memset(q_st[p][:].bitcast(U32), 0)
                nc.gpsimd.memset(k_st[p][:].bitcast(U32), 0)
            nc.gpsimd.memset(m_zero[:].bitcast(U32), 0).then_inc(const_step, 1)
            pool.wait_ge(const_step, 6)
            for p in range(2):
                last = nc.gpsimd.memset(k_st[p][SH:ROWS, :, :], 1.0)
            last.then_inc(stacks_clear, 1)
            pool.wait_ge(stacks_clear, 1)

            for c in range(C):
                pool.wait_ge(y_used[0], c + 1)
                nc.gpsimd.tensor_tensor(x_b[:, chunk(c), :], x_1[:, chunk(c), :],
                                        bo_row[:].unsqueeze(1).to_broadcast([P, TC, D]), ALU.add).then_inc(xb2_ready, 1)

            pool.wait_ge(v_used, C)
            with pool.Fori(0, PAIRS) as i:
                for p in range(2):
                    pool.wait_ge(v_st_used[p], i + 1)
                    nc.gpsimd.tensor_copy(v_st[p][:], v_aug[:, bass.ds(i * 2 + p, 1)].rearrange("p g k v -> p (g k) v")
                                          ).then_inc(v_staged[p], 1)

            for c in range(C):
                pool.wait_ge(o_used, c + 1)
                nc.gpsimd.tensor_tensor(x_b[:, chunk(c), :], x_2[:, chunk(c), :],
                                        b2h_row[:].unsqueeze(1).to_broadcast([P, TC, D]), ALU.add).then_inc(xb3_ready, 1)

        @block.scalar
        def _(act):
            count = [0]

            def done(ins):
                count[0] += 1
                ins.then_inc(act_step, 1)
                act.wait_ge(act_step, count[0])

            act.dma_start(wq_sb[:], Wq).then_inc(attn_w_loaded, 16)
            act.dma_start(wk_sb[:], Wk).then_inc(attn_w_loaded, 16)
            act.dma_start(wv_sb[:], Wv).then_inc(attn_w_loaded, 16)
            act.dma_start(bv_row[:], bv.partition_broadcast(P)).then_inc(attn_w_loaded, 16)
            act.dma_start(bg_row[:], bq[D:D + H].partition_broadcast(P)).then_inc(attn_w_loaded, 16)
            act.dma_start(qn_row[:], qn_w.partition_broadcast(P)).then_inc(r_w_loaded, 16)
            act.dma_start(kn_row[:], kn_w.partition_broadcast(P)).then_inc(r_w_loaded, 16)
            act.dma_start(wo_sb[:], Wo).then_inc(wo_loaded, 16)

            def inverse_std(stage, group):
                t = slice(group[0] * TC, (group[-1] + 1) * TC)
                act.wait_ge(stats_ready[stage], group[-1] + 1)
                done(nc.scalar.activation(ln_var[:, t], mean_var[:, t, 1], ACT.Ln, bias=eps[:, 0:1]))
                nc.scalar.activation(rstd[:, t], ln_var[:, t], ACT.Exp, scale=-0.5).then_inc(rstd_ready[stage], 1)

            def copy_xnT(stage, c):
                act.wait_ge(xnT_psum[stage], c + 1)
                nc.scalar.copy(x_nT[:, cols(c)], ps[:, 4, :]).then_inc(xnT_ready[stage], 1)

            def gelu(f, c):
                if c >= 2:
                    act.wait_ge(y_psum[f], c - 1)
                for m in range(M):
                    act.wait_ge(h_psum[f], M * c + m + 1)
                    nc.scalar.activation(hT[:, c % 2, m, :], ps[:, m, :], ACT.Gelu,
                                         bias=b1_col[:, m:m + 1]).then_inc(h_ready[f], 1)

            nc.scalar.preload_act_table_set("natural_log_exp_and_others")
            act.wait_ge(consts_ready, 2)
            for g in RSTD_GROUPS[0]:
                inverse_std(0, g)
            act.wait_ge(vec_ready, 1)
            copy_xnT(0, 0)
            for c in range(C):
                if c + 1 < C:
                    copy_xnT(0, c + 1)
                gelu(0, c)
            nc.scalar.preload_act_table_set("natural_log_exp_and_others")
            for g in RSTD_GROUPS[1]:
                inverse_std(1, g)

            act.wait_ge(attn_w_loaded, 16 * 5)
            copy_xnT(1, 0)
            for c in range(C):
                for s in range(2):
                    act.wait_ge(sum_ready, 2 * c + s + 1)
                    nc.scalar.activation(qk_sq[:, s, :], qk_sum[:, s, :], ACT.Square).then_inc(sq_ready, 1)
                if c + 1 < C:
                    copy_xnT(1, c + 1)
                for s in range(2):
                    act.wait_ge(ms_psum, 2 * c + s + 1)
                    if c >= 1:
                        act.wait_ge(r_ready, 2 * c - 1 + s)
                    ins = nc.scalar.activation(qk_ln[:, s, :], ps[:, 6 + s, :], ACT.Ln, bias=eps[:, 1:2])
                    ins.then_inc(ln_done, 1)
                    act.wait_ge(ln_done, 2 * c + s + 1)
                    if c >= 1:
                        act.wait_ge(norm_ready, 2 * c - 1 + s)
                    nc.scalar.activation(qk_r[:, s, :], qk_ln[:, s, :], ACT.Exp, scale=-0.5).then_inc(r_ready, 1)
            act.wait_ge(gate_sum, 1)
            nc.scalar.activation(gate[:], gate[:], ACT.Exp, scale=-1.0).then_inc(gate_exp, 1)

            act.wait_ge(v_used, C)
            act.wait_ge(gate_sum, 1)
            act.sem_inc(probs_ready, FREE3)

            def exp_tiles(i, first, last):
                for n in range(first, last):
                    act.wait_ge(scores_ready, i * BT + n + 1)
                    act.wait_ge(pv_done, i * (BT // 2) + n // 2 + 1)
                    b = SBUF_OF[n]
                    nc.scalar.activation(probs[:, n % PB, :], ps[:, 2 * b:2 * b + 2, :].rearrange("p b n -> p (b n)"),
                                         ACT.Exp).then_inc(probs_ready, 1)

            with act.Fori(0, PAIRS) as i:
                exp_tiles(i, 0, BT)

            def copy_oT(c):
                act.wait_ge(oT_psum, c + 1)
                nc.scalar.copy(oT[:, cols(c)], ps[:, 4, :]).then_inc(oT_ready, 1)

            for c in range(C):
                copy_oT(c)
            for g in RSTD_GROUPS[2]:
                inverse_std(2, g)
            copy_xnT(2, 0)
            for c in range(C):
                if c + 1 < C:
                    copy_xnT(2, c + 1)
                gelu(1, c)

        @block.vector
        def _(dve):
            count = [0]

            def done(ins):
                count[0] += 1
                ins.then_inc(dve_step, 1)
                dve.wait_ge(dve_step, count[0])

            def token_stats(stage, src, c):
                for t in range(c * TC, (c + 1) * TC):
                    last = nc.vector.bn_stats(stats[:, t, :], src[:, t, :])
                done(last)
                for t in range(c * TC, (c + 1) * TC):
                    last = nc.vector.bn_aggr(mean_var[:, t, :], stats[:, t, :])
                last.then_inc(stats_ready[stage], 1)

            def normalise(stage, src, c):
                dve.wait_ge(rstd_ready[stage], rstd_group(stage, c) + 1)
                dve.wait_ge(stats_ready[stage], c + 1)
                for t in range(c * TC, (c + 1) * TC):
                    last = nc.vector.tensor_scalar(x_n[:, t, :], src[:, t, :], mean_var[:, t, 0:1], rstd[:, t:t + 1],
                                                   ALU.subtract, ALU.mult)
                last.then_inc(xn_ready[stage], 1)

            for c in range(C):
                if c == 1:
                    dve.wait_ge(vec_psum, 1)
                    nc.vector.tensor_copy(vec_cols[:], ps[:, 7, 0:M + 4]).then_inc(vec_ready, 1)
                dve.wait_ge(x_loaded[c], 16)
                token_stats(0, x_in, c)
                if c >= 1:
                    normalise(0, x_in, c - 1)
            normalise(0, x_in, C - 1)

            dve.wait_ge(r_w_loaded, 16 * 2)
            dve.wait_ge(vec_ready, 1)
            done(nc.vector.tensor_scalar(qs_col[:], qn_col, float(HD) ** -0.5, None, ALU.mult))
            done(nc.vector.tensor_tensor(r_w[:, 0, :], qn_row[:], kn_row[:], ALU.mult))
            done(nc.vector.tensor_scalar(r_w[:, 1, :], r_w[:, 0, :], -1.0, None, ALU.mult))
            done(nc.vector.tensor_tensor(r_w[:, 2, :], r_w[:, 0, :], r_w[:, 1, :], ALU.max))
            done(nc.vector.reduce_max(r_col[:, 0:1], r_w[:, 2, :], AX_X))
            done(nc.vector.tensor_scalar(r_col[:, 1:2], r_col[:, 0:1], -float(HD) ** 0.5, None, ALU.mult))
            nc.vector.tensor_scalar(flag[:], r_col[:, 1:2], -SHIFT_SAFE, None, ALU.is_lt).then_inc(r_known, 1)
            done(nc.vector.tensor_copy(r_bf[:, 0:1], r_col[:, 1:2]))
            done(nc.vector.tensor_tensor(r_col[:, 2:3], r_col[:, 1:2], r_bf[:, 0:1], ALU.subtract))
            done(nc.vector.tensor_copy(r_bf[:, 1:2], r_col[:, 2:3]))
            done(nc.vector.tensor_tensor(r_col[:, 3:4], r_col[:, 2:3], r_bf[:, 1:2], ALU.subtract))
            for s, part in enumerate((r_bf[0:1, 0:1], r_bf[0:1, 1:2], r_col[0:1, 3:4])):
                last = nc.vector.tensor_copy(r_rows[0:1, s, :], part.to_broadcast([1, N]))
            last.then_inc(r_rows_ready, 1)

            for c in range(C):
                dve.wait_ge(xb_ready, c + 1)
                dve.wait_ge(y_psum[0], c + 1)
                ins = nc.vector.scalar_tensor_tensor(
                    out=x_1[:, chunk(c), :].rearrange("p t d -> p (t d)"), in0=ps[:, 5, :], scalar=0.5,
                    in1=x_b[:, chunk(c), :].rearrange("p t d -> p (t d)"), op0=ALU.mult, op1=ALU.add)
                ins.then_inc(y_used[0], 1)
                dve.wait_ge(y_used[0], c + 1)
                token_stats(1, x_1, c)
            normalise(1, x_1, 0)

            dve.wait_ge(attn_w_loaded, 16 * 5)
            dve.wait_ge(ones_ready, 1)
            for c in range(C):
                for s, b_col in ((0, bq_col), (1, bk_col)):
                    dve.wait_ge(qk_psum, 2 * c + s + 1)
                    if c >= 1:
                        dve.wait_ge(sq_ready, 2 * c - 1 + s)
                    nc.vector.tensor_scalar(qk_sum[:, s, :], ps[:, 6 + s, :], b_col[:, 0:1], None,
                                            ALU.add).then_inc(sum_ready, 1)
                if c + 1 < C:
                    normalise(1, x_1, c + 1)
                dve.wait_ge(v_psum, c + 1)
                for tl in range(TC):
                    b, kt = divmod(c * TC + tl, KT)
                    last = nc.vector.tensor_tensor(
                        v_aug[:, b * GB:(b + 1) * GB, kt, :].rearrange("p g (j v) -> p g j v", v=VW)[:, :, :, 0:HD],
                        ps[:, 5, tl * D:(tl + 1) * D].rearrange("p (g j d) -> p g j d", j=HG, d=HD),
                        bv_row[:].rearrange("p (g j d) -> p g j d", j=HG, d=HD), ALU.add)
                last.then_inc(v_used, 1)
                for s, w_col in ((0, qs_col), (1, kn_col)):
                    dve.wait_ge(r_ready, 2 * c + s + 1)
                    nc.vector.scalar_tensor_tensor(out=qk_n[:, s, :], in0=qk_sum[:, s, :], scalar=w_col[:, 0:1],
                                                   in1=qk_r[:, s, :], op0=ALU.mult, op1=ALU.mult
                                                   ).then_inc(norm_ready, 1)
                    dve.wait_ge(norm_ready, 2 * c + s + 1)
                    done(nc.vector.tensor_copy(parts[:, s, 0, cols(c)], qk_n[:, s, :]))
                    done(nc.vector.tensor_tensor(qk_rest[:, s, :], qk_n[:, s, :], parts[:, s, 0, cols(c)],
                                                 ALU.subtract))
                    done(nc.vector.tensor_copy(parts[:, s, 1, cols(c)], qk_rest[:, s, :]))
                    nc.vector.tensor_tensor(parts[:, s, 2, cols(c)], qk_rest[:, s, :], parts[:, s, 1, cols(c)],
                                            ALU.subtract).then_inc(parts_ready, 1)
            dve.wait_ge(gate_psum, 1)
            nc.vector.tensor_tensor(gate[:], ps[:, 0, 0:T * H].rearrange("p (t h) -> p t h", h=H),
                                    bg_row[:].unsqueeze(1).to_broadcast([P, T, H]), ALU.add).then_inc(gate_sum, 1)
            dve.wait_ge(gate_exp, 1)
            done(nc.vector.tensor_scalar(gate[:], gate[:], 1.0, None, ALU.add))
            for b in range(B):
                last = nc.vector.reciprocal(
                    sig[:, b * GB:(b + 1) * GB, :, :],
                    gate[:, b * KT:(b + 1) * KT, :].rearrange("p t (g j) -> p g t j", j=HG))
            last.then_inc(sig_ready, 1)

            dve.wait_ge(r_known, 1)
            large = dve.value_load(flag[0:1, 0:1], min_val=0, max_val=1)
            U = HG * KT
            with dve.If(large > 0):
                dve.sem_inc(ex_parts, 1)
                with dve.Fori(0, G) as g:
                    for u in range(U):
                        dve.wait_ge(ex_scores, g * U + u + 1)
                        nc.vector.reduce_max(mx[:, u:u + 1], ps[:, 2 * (u % 2):2 * (u % 2) + 2, :]
                                             .rearrange("p b n -> p (b n)"), AX_X).then_inc(ex_max, 1)
                    dve.wait_ge(ex_mT, g + 1)
                    nc.vector.tensor_scalar(mx_n[:], ps[0:U, 4, 0:P], -1.0, None, ALU.mult).then_inc(ex_step, 1)
                    dve.wait_ge(ex_step, g * 4 + 1)
                    dve.wait_ge(ex_stored, g * 16 + 16)
                    nc.vector.tensor_copy(mx_parts[:, 0, :], mx_n[:]).then_inc(ex_step, 1)
                    dve.wait_ge(ex_step, g * 4 + 2)
                    nc.vector.tensor_tensor(mx_r[:], mx_n[:], mx_parts[:, 0, :], ALU.subtract).then_inc(ex_step, 1)
                    dve.wait_ge(ex_step, g * 4 + 3)
                    nc.vector.tensor_copy(mx_parts[:, 1, :], mx_r[:]).then_inc(ex_step, 1)
                    dve.wait_ge(ex_step, g * 4 + 4)
                    nc.vector.tensor_tensor(mx_parts[:, 2, :], mx_r[:], mx_parts[:, 1, :],
                                            ALU.subtract).then_inc(ex_parts, 1)

            dve.wait_ge(sig_ready, 1)
            dve.sem_inc(o_ready, FREE2)

            def finish(b, i, k):
                half = k % 2
                bank = ACC + half
                item = (b * (GB // 2) + i) * 4 + k
                g = b * GB + i * 2 + k // 2
                heads = bass.ds((i * 2 + k // 2) * (HG * HD), HG * HD)
                dve.wait_ge(pv_done, item * KT + KT + PB // 2)
                nc.vector.tensor_copy(acc_sb[:, half, :], ps[:, bank, :]).then_inc(acc_copied, 1)
                dve.wait_ge(accT_psum, item + 1)
                rows = ps[:, bank, :].rearrange("p (t j v) -> p t j v", j=HG, v=32)
                nc.vector.reciprocal(r_den[:], rows[:, :, :, HD]).then_inc(norm_step, 1)
                dve.wait_ge(norm_step, item * 2 + 1)
                nc.vector.tensor_tensor(fac[:], r_den[:], sig[:, bass.ds(g, 1), 4 * half:4 * half + 4, :]
                                        .rearrange("p g t j -> p (g t) j"), ALU.mult).then_inc(norm_step, 1)
                dve.wait_ge(norm_step, item * 2 + 2)
                nc.vector.tensor_tensor(
                    o_nat[:, bass.ds(b * KT + 4 * half, 4), heads].rearrange("p t (j d) -> p t j d", d=HD),
                    rows[:, :, :, 0:HD], fac[:].unsqueeze(3).to_broadcast([P, 4, HG, HD]),
                    ALU.mult).then_inc(o_ready, 1)

            with dve.Fori(0, B) as b:
                with dve.Fori(0, GB // 2) as i:
                    for k in range(4):
                        finish(b, i, k)

            for c in range(C):
                dve.wait_ge(xb2_ready, c + 1)
                dve.wait_ge(o_psum, c + 1)
                nc.vector.tensor_tensor(x_2[:, chunk(c), :].rearrange("p t d -> p (t d)"), ps[:, 5, :],
                                        x_b[:, chunk(c), :].rearrange("p t d -> p (t d)"), ALU.add).then_inc(o_used, 1)
                dve.wait_ge(o_used, c + 1)
                token_stats(2, x_2, c)
            for c in range(C):
                normalise(2, x_2, c)
            for c in range(C):
                dve.wait_ge(xb3_ready, c + 1)
                dve.wait_ge(y_psum[1], c + 1)
                nc.vector.scalar_tensor_tensor(
                    out=y_out[:, chunk(c), :].rearrange("p t d -> p (t d)"), in0=ps[:, 5, :], scalar=0.5,
                    in1=x_b[:, chunk(c), :].rearrange("p t d -> p (t d)"), op0=ALU.mult, op1=ALU.add
                ).then_inc(out_ready, 1)

        @block.tensor
        def _(pe):
            def transpose_xn(stage, c):
                pe.wait_ge(xn_ready[stage], c + 1)
                if c >= 1:
                    pe.wait_ge(xnT_ready[stage], c)
                for tl in range(TC):
                    last = nc.tensor.transpose(ps[:, 4, tl * P:(tl + 1) * P], x_n[:, c * TC + tl, :], ident[:])
                last.then_inc(xnT_psum[stage], 1)

            def ffn_in(f, stage, c):
                pe.wait_ge(xnT_ready[stage], c + 1)
                for m in range(M):
                    if c >= 1:
                        pe.wait_ge(h_ready[f], M * (c - 1) + m + 1)
                    nc.tensor.matmul(ps[:, m, :], w1_sb[:, m * P:(m + 1) * P], x_nT[:, cols(c)],
                                     start=True, stop=True).then_inc(h_psum[f], 1)

            def ffn_out(f, c, used):
                pe.wait_ge(h_ready[f], M * (c + 1))
                if c >= 1:
                    pe.wait_ge(used, c)
                for tl in range(TC):
                    for m in range(M):
                        last = nc.tensor.matmul(ps[:, 5, tl * D:(tl + 1) * D], hT[:, c % 2, m, tl * P:(tl + 1) * P],
                                                w2_sb[:, m, :], start=(m == 0), stop=(m == M - 1))
                last.then_inc(y_psum[f], 1)

            def ffn(f, stage, used):
                transpose_xn(stage, 0)
                ffn_in(f, stage, 0)
                for c in range(1, C):
                    transpose_xn(stage, c)
                    ffn_in(f, stage, c)
                    ffn_out(f, c - 1, used)
                ffn_out(f, C - 1, used)

            pe.wait_ge(consts_ready, 1)
            pe.wait_ge(vec_loaded, 16 * 5)
            nc.tensor.transpose(ps[:, 7, 0:M + 4], vec_rows[:], ident[0:M + 4, 0:M + 4]).then_inc(vec_psum, 1)
            pe.wait_ge(consts_ready, 2)
            pe.wait_ge(w1_loaded, 16)
            pe.wait_ge(w2_loaded, 16)
            ffn(0, 0, y_used[0])

            pe.wait_ge(attn_w_loaded, 16 * 5)
            pe.wait_ge(y_used[0], C)
            transpose_xn(1, 0)
            for c in range(C):
                pe.wait_ge(xnT_ready[1], c + 1)
                for s, w in ((0, wq_sb[:, 0:D]), (1, wk_sb[:])):
                    if c >= 1:
                        pe.wait_ge(ln_done, 2 * c - 1 + s)
                    nc.tensor.matmul(ps[:, 6 + s, :], w, x_nT[:, cols(c)], start=True, stop=True).then_inc(qk_psum, 1)
                if c >= 1:
                    pe.wait_ge(v_used, c)
                for tl in range(TC):
                    t = c * TC + tl
                    nc.tensor.matmul(ps[:, 0, t * H:(t + 1) * H], x_nT[:, t * P:(t + 1) * P], wq_sb[:, D:D + H],
                                     start=True, stop=True)
                    last = nc.tensor.matmul(ps[:, 5, tl * D:(tl + 1) * D], x_nT[:, t * P:(t + 1) * P], wv_sb[:],
                                            start=True, stop=True)
                last.then_inc(v_psum, 1)
                if c + 1 < C:
                    transpose_xn(1, c + 1)
                for s in range(2):
                    pe.wait_ge(sq_ready, 2 * c + s + 1)
                    last = nc.tensor.matmul(ps[:, 6 + s, :], head_mean[:], qk_sq[:, s, :], start=True, stop=True)
                    last.then_inc(ms_psum, 1)
                if c == C - 1:
                    pe.wait_ge(ms_psum, 2 * C)
                    pe.sem_inc(gate_psum, 1)

            pe.wait_ge(v_used, C)
            pe.wait_ge(gate_sum, 1)
            pe.wait_ge(xnT_ready[1], C)

            pe.wait_ge(r_known, 1)
            large = pe.value_load(flag[0:1, 0:1], min_val=0, max_val=1)
            U = HG * KT
            with pe.If(large > 0):
                pe.sem_inc(ex_max, 2)
                with pe.Fori(0, G) as g:
                    pe.wait_ge(ex_loaded, g * (16 * LOADS) + 16 * LOADS)
                    for u in range(U):
                        j, qt = divmod(u, KT)
                        pe.wait_ge(ex_max, g * U + u + 1)
                        for h in range(2):
                            last = nc.tensor.matmul(ps[:, 2 * (u % 2) + h, :], q_st[0][0:ROWS, j, qt * P:(qt + 1) * P],
                                                    k_st[0][0:ROWS, j, h * 512:(h + 1) * 512], start=True, stop=True)
                        last.then_inc(ex_scores, 1)
                    pe.wait_ge(ex_max, g * U + U + 2)
                    nc.tensor.transpose(ps[0:U, 4, 0:P], mx[:], ident[:]).then_inc(ex_mT, 1)
                pe.wait_ge(ex_parts, G + 1)

            pe.sem_inc(pv_done, PB // 2)
            for p in range(2):
                pe.sem_inc(stack_used[p], 1)
                pe.sem_inc(v_st_used[p], 1)

            def scores(i, n, wait=True):
                p, m = divmod(n % BT, TILES)
                step, jj = divmod(m, 2)
                half, kt = divmod(step, KT)
                if m == 0:
                    pe.wait_ge(stack_loaded[p], (i + n // BT) * (16 * LOADS) + 16 * LOADS)
                pe.wait_ge(probs_ready, i * BT + (n - n % BT) + PREV[n % BT] + 1 + FREE3)
                for u in range(2):
                    j = 2 * jj + u
                    last = nc.tensor.matmul(ps[:, 2 * SBUF_OF[n % BT] + u, :],
                                            k_st[p][0:ROWS, j, kt * P:(kt + 1) * P],
                                            q_st[p][0:ROWS, j, half * 512:(half + 1) * 512], start=True, stop=True)
                last.then_inc(scores_ready, 1)
                if m == TILES - 1:
                    pe.wait_ge(scores_ready, i * BT + n + 1)
                    pe.sem_inc(stack_used[p], 1)

            def weighted(i, s):
                p, step = divmod(s, STEPS)
                half, kt = divmod(step, KT)
                if step == 0:
                    pe.wait_ge(v_staged[p], i + 1)
                if kt == 0:
                    pe.wait_ge(o_ready, i * 4 + 2 * p + half + 1)
                pe.wait_ge(probs_ready, i * BT + 2 * s + 2 + FREE3)
                for j in range(HG):
                    last = nc.tensor.matmul(ps[32 * j:32 * j + VW, ACC + half, :],
                                            v_st[p][:, kt, j * VW:(j + 1) * VW],
                                            probs[:, (2 * s + j // 2) % PB, (j % 2) * 512:(j % 2 + 1) * 512],
                                            start=(kt == 0), stop=(kt == KT - 1))
                last.then_inc(pv_done, 1)

            def turn(i, k):
                half = k % 2
                pe.wait_ge(acc_copied, i * 4 + k + 1)
                for t in range(4):
                    last = nc.tensor.transpose(ps[:, ACC + half, t * P:(t + 1) * P],
                                               acc_sb[:, half, t * P:(t + 1) * P], ident[:])
                last.then_inc(accT_psum, 1)

            def iteration(i, final):
                for s in range(2 * STEPS):
                    if not (final and 2 * s + 4 >= BT):
                        scores(i, 2 * s + 4)
                    weighted(i, s)
                    if s == STEPS - 1 or s == 2 * STEPS - 1:
                        pe.wait_ge(pv_done, i * (2 * STEPS) + s + 1 + PB // 2)
                        pe.sem_inc(v_st_used[s // STEPS], 1)
                    if not (final and 2 * s + 5 >= BT):
                        scores(i, 2 * s + 5)
                    if s % KT == 1 and s > KT:
                        turn(i, s // KT - 1)
                turn(i, 3)

            for n in range(4):
                scores(0, n)
            with pe.Fori(0, PAIRS - 1) as i:
                iteration(i, False)
            iteration(PAIRS - 1, True)

            pe.wait_ge(wo_loaded, 16)
            pe.wait_ge(o_ready, 2 * G + FREE2)
            for c in range(C):
                if c >= 1:
                    pe.wait_ge(oT_ready, c)
                for tl in range(TC):
                    last = nc.tensor.transpose(ps[:, 4, tl * P:(tl + 1) * P], o_nat[:, c * TC + tl, :], ident[:])
                last.then_inc(oT_psum, 1)
                pe.wait_ge(oT_ready, c + 1)
                if c >= 1:
                    pe.wait_ge(o_used, c)
                for tl in range(TC):
                    t = c * TC + tl
                    last = nc.tensor.matmul(ps[:, 5, tl * D:(tl + 1) * D], oT[:, t * P:(t + 1) * P], wo_sb[:],
                                            start=True, stop=True)
                last.then_inc(o_psum, 1)

            pe.wait_ge(o_used, C)
            ffn(1, 2, out_ready)


_INS = ["L0_attn_x", "L0_attn_Wq", "L0_attn_bq", "L0_attn_Wk", "L0_attn_bk", "L0_attn_Wv", "L0_attn_bv",
        "L0_attn_Wo", "L0_attn_bo", "L0_attn_qn_w", "L0_attn_kn_w", "L0_ffn_w1", "L0_ffn_b1", "L0_ffn_w2",
        "L0_ffn_b2"]
_OUTS = [((2, 1024, 128), "float32")]


def kernel(**inputs):
    import numpy as _np
    import concourse.bacc as _bacc
    from concourse import mybir as _mybir
    from concourse.bass_utils import run_bass_kernel_spmd as _run

    nc = _bacc.Bacc("TRN2", target_bir_lowering=False, num_devices=1)
    arrays, args = {}, []
    for name in _INS:
        a = _np.ascontiguousarray(inputs[name])
        arrays[f"in_{name}"] = a
        args.append(nc.dram_tensor(f"in_{name}", a.shape, _mybir.dt.from_np(a.dtype), kind="ExternalInput").ap())
    for i, (shape, dtype) in enumerate(_OUTS):
        dt = _mybir.dt.from_np(_np.dtype(dtype))
        args.append(nc.dram_tensor(f"out_{i}", shape, dt, kind="ExternalOutput").ap())
    macaron_kernel(nc, *args)
    r = _run(nc, [arrays], core_ids=[0])
    got = tuple(r.results[0][f"out_{i}"] for i in range(len(_OUTS)))
    return got[0]
```

```python
from contextlib import ExitStack

import numpy as np

import concourse.bass as bass
from concourse import mybir

F32 = mybir.dt.float32
BF16 = mybir.dt.bfloat16
I32 = mybir.dt.int32
U32 = mybir.dt.uint32
ALU = mybir.AluOpType
ACT = mybir.ActivationFunctionType
AX_X = mybir.AxisListType.X

LN_EPS = 1e-5
RMS_EPS = 1e-6
ONES = 0x3F803F80
SHIFT_SAFE = 30.0


def macaron_kernel(nc, x, Wq, bq, Wk, bk, Wv, bv, Wo, bo, qn_w, kn_w, w1, b1, w2, b2, out):
    P = 128
    B, N, D = x.shape
    H = Wq.shape[1] - D
    HD = D // H
    F = w1.shape[1]
    T = B * N // P
    C = B * N // 512
    TC = T // C
    M = F // P
    assert (P, D, HD, TC, T, M) == (128, 128, 8, 4, 16, 4)
    HG = 4
    G = B * H // HG
    GB = G // B
    KT = N // P
    VW = HD + 1
    PAIRS = G // 2
    PROD = 9 * HD
    SH = 96
    ROWS = SH + 6
    STEPS = 2 * KT
    TILES = 2 * STEPS
    BT = 2 * TILES
    SBUF_OF = [0, 1, 2] * ((BT - 4) // 3) + [0, 1, 0, 2]
    PREV = [max([m for m in range(-BT, n) if SBUF_OF[m % BT] == SBUF_OF[n]]) for n in range(BT)]
    FREE3 = 3
    FREE2 = 2
    PB = 8
    ACC = 6
    LOADS = 5

    with ExitStack() as ctx:
        def sb(name, shape, dt=F32):
            return ctx.enter_context(nc.sbuf_tensor(name, shape, dt))

        def sem(name):
            return ctx.enter_context(nc.semaphore(name))

        ps = ctx.enter_context(nc.psum_tensor("ps", [P, 8, 512], F32))

        w1_sb = sb("w1_sb", [P, F])
        w2_sb = sb("w2_sb", [P, M, D])
        wq_sb = sb("wq_sb", [P, D + H])
        wk_sb = sb("wk_sb", [P, D])
        wv_sb = sb("wv_sb", [P, D])
        wo_sb = sb("wo_sb", [P, D])
        vec_rows = sb("vec_rows", [M, P])
        qk_rows = sb("qk_rows", [4, P])
        qk_rows_p = sb("qk_rows_p", [4, P])
        wqk_p = sb("wqk_p", [P, 2, D])
        head_sum = sb("head_sum", [P, H])
        vec_cols = sb("vec_cols", [P, M + 4])
        b1_col = vec_cols[:, 0:M]
        bq_col, bk_col, qn_col, kn_col = (vec_cols[:, M + n:M + n + 1] for n in range(4))
        qk_w_col = sb("qk_w_col", [P, 2])
        qk_bw_col = sb("qk_bw_col", [P, 2])
        b2_row = sb("b2_row", [P, D])
        b2h_row = sb("b2h_row", [P, D])
        bo_row = sb("bo_row", [P, D])
        bv_row = sb("bv_row", [P, D])
        bg_row = sb("bg_row", [P, H])
        qn_row = sb("qn_row", [P, HD])
        kn_row = sb("kn_row", [P, HD])
        ident = sb("ident", [P, P])
        head_mean = sb("head_mean", [P, P])
        eps = sb("eps", [P, 1])
        x_in = sb("x_in", [P, T, D])
        x_b = sb("x_b", [P, T, D])
        x_1 = sb("x_1", [P, T, D])
        x_2 = sb("x_2", [P, T, D])
        y_out = x_in
        x_n = sb("x_n", [P, T, D])
        stats = sb("stats", [P, T, 6])
        mean_var = sb("mean_var", [P, T, 2])
        var_eps = sb("var_eps", [P, T])
        minus_half = sb("minus_half", [P, T])
        rstd = sb("rstd", [P, T])
        x_nT = sb("x_nT", [P, T * P])
        oT = x_nT
        qk = sb("qk", [P, C, 2, 512])
        qk_sq = sb("qk_sq", [P, 2, 512])
        qk_ms = sb("qk_ms", [P, C, 2, 512])
        parts = sb("parts", [P, 2, 3, N], BF16)
        v_aug = sb("v_aug", [P, G, KT, HG * VW])
        gate = sb("gate", [P, T, H])
        sig = sb("sig", [P, G, KT, HG])
        r_w = sb("r_w", [P, 4, HD])
        r_col = sb("r_col", [P, 8])
        r_bf = sb("r_bf", [P, 2], BF16)
        r_rows = sb("r_rows", [P, 3, N], BF16)
        flag = sb("flag", [P, 1], I32)
        q_st = [sb(f"q_st{p}", [P, HG, N], BF16) for p in range(2)]
        k_st = [sb(f"k_st{p}", [P, HG, N], BF16) for p in range(2)]
        v_st = [sb(f"v_st{p}", [P, KT, HG * VW]) for p in range(2)]
        probs = sb("probs", [P, PB, 1024])
        hT = probs[:, 0:4, :].rearrange("p (c m) (h n) -> p c (m h) n", c=2, h=2)
        acc_sb = sb("acc_sb", [P, 2, 512])
        r_den = sb("r_den", [P, 4, HG])
        fac = sb("fac", [P, 4, HG])
        o_nat = sb("o_nat", [P, T, D])
        mx = sb("mx", [P, HG * KT])
        mx_n = sb("mx_n", [HG * KT, P])
        mx_r = sb("mx_r", [HG * KT, P])
        mx_parts = sb("mx_parts", [HG * KT, 3, P], BF16)
        m_zero = acc_sb[:, 0, :].bitcast(BF16)

        part_dram = [nc.dram_tensor(f"part_dram{s}", [G, 3, HD * HG, N], BF16, kind="Internal").ap() for s in range(2)]
        m_dram = nc.dram_tensor("m_dram", [G, 3, HG * N], BF16, kind="Internal").ap()

        x_loaded = [sem(f"x_loaded{c}") for c in range(C)]
        w1_loaded = sem("w1_loaded")
        w2_loaded = sem("w2_loaded")
        vec_loaded = sem("vec_loaded")
        vec_psum = sem("vec_psum")
        vec_ready = sem("vec_ready")
        qk_rows_loaded = sem("qk_rows_loaded")
        qk_rows_ready = sem("qk_rows_ready")
        qk_w_ready = sem("qk_w_ready")
        attn_w_loaded = sem("attn_w_loaded")
        rows_loaded = sem("rows_loaded")
        r_w_loaded = sem("r_w_loaded")
        wo_loaded = sem("wo_loaded")
        const_step = sem("const_step")
        consts_ready = sem("consts_ready")
        xb_ready = sem("xb_ready")
        xb2_ready = sem("xb2_ready")
        xb3_ready = sem("xb3_ready")
        stats_ready = [sem(f"stats_ready{k}") for k in range(3)]
        var_ready = sem("var_ready")
        rstd_ready = [sem(f"rstd_ready{k}") for k in range(3)]
        xn_ready = [sem(f"xn_ready{k}") for k in range(3)]
        turned = sem("turned")
        turned_copied = sem("turned_copied")
        h_psum = [sem(f"h_psum{k}") for k in range(2)]
        h_ready = [sem(f"h_ready{k}") for k in range(2)]
        y_psum = [sem(f"y_psum{k}") for k in range(2)]
        y_used = [sem(f"y_used{k}") for k in range(2)]
        dve_step = sem("dve_step")
        qk_psum = sem("qk_psum")
        v_psum = sem("v_psum")
        v_used = sem("v_used")
        gate_psum = sem("gate_psum")
        gate_sum = sem("gate_sum")
        gate_exp = sem("gate_exp")
        sig_ready = sem("sig_ready")
        sum_ready = sem("sum_ready")
        ms_psum = sem("ms_psum")
        ms_ready = sem("ms_ready")
        ln_ready = sem("ln_ready")
        r_ready = sem("r_ready")
        qk_scaled = sem("qk_scaled")
        parts_ready = sem("parts_ready")
        ones_ready = sem("ones_ready")
        r_known = sem("r_known")
        r_rows_ready = sem("r_rows_ready")
        stacks_clear = sem("stacks_clear")
        parts_stored = [sem(f"parts_stored{s}") for s in range(2)]
        m_stored = sem("m_stored")
        shift_rows_loaded = sem("shift_rows_loaded")
        ex_loaded = sem("ex_loaded")
        ex_scores = sem("ex_scores")
        ex_max = sem("ex_max")
        ex_mT = sem("ex_mT")
        ex_step = sem("ex_step")
        ex_parts = sem("ex_parts")
        ex_stored = sem("ex_stored")
        stack_loaded = [sem(f"stack_loaded{p}") for p in range(2)]
        v_staged = [sem(f"v_staged{p}") for p in range(2)]
        scores_ready = sem("scores_ready")
        probs_ready = sem("probs_ready")
        pv_done = sem("pv_done")
        acc_copied = sem("acc_copied")
        accT_psum = sem("accT_psum")
        norm_step = sem("norm_step")
        o_ready = sem("o_ready")
        o_psum = sem("o_psum")
        o_used = sem("o_used")
        out_ready = sem("out_ready")
        out_stored = sem("out_stored")

        x_dram = x.rearrange("b (t p) d -> p (b t) d", p=P)
        out_dram = out.rearrange("b (t p) d -> p (b t) d", p=P)

        def chunk(c):
            return slice(c * TC, (c + 1) * TC)

        def cols(c):
            return slice(c * 512, (c + 1) * 512)

        def h_bank(m):
            return ps[:, m % 2, :]

        def t_bank(n):
            return ps[:, 2 + n % 2, :]

        Y_BANK, V_BANK, Q_BANK, GATE_BANK = 4, 5, 6, 0

        def per_head(w):
            return bass.AP(w.tensor, w.offset, [[0, 1], [0, H], [1, HD]])

        block = ctx.enter_context(nc.Block())

        @block.sync
        def _(sp):
            for c in range(C):
                sp.dma_start(x_in[:, chunk(c), :], x_dram[:, chunk(c), :]).then_inc(x_loaded[c], 16)
                if c == 0:
                    sp.dma_start(w1_sb[:], w1).then_inc(w1_loaded, 16)
            sp.dma_start(w2_sb[:], w2.rearrange("(m p) e -> p m e", p=P)).then_inc(w2_loaded, 16)
            sp.dma_start(b2_row[:], b2.partition_broadcast(P)).then_inc(rows_loaded, 16)
            sp.dma_start(bo_row[:], bo.partition_broadcast(P)).then_inc(rows_loaded, 16)
            sp.dma_start(bv_row[:], bv.partition_broadcast(P)).then_inc(attn_w_loaded, 16)
            sp.dma_start(bg_row[:], bq[D:D + H].partition_broadcast(P)).then_inc(attn_w_loaded, 16)
            sp.dma_start(wo_sb[:], Wo).then_inc(wo_loaded, 16)

            def store_parts(s, b):
                for part in range(3):
                    sp.wait_ge(parts_ready, 3 * (4 * b + 2 * s + 1) + part + 1)
                    sp.dma_start(part_dram[s][b * GB:(b + 1) * GB, part], parts[:, s, part, :]
                                 ).then_inc(parts_stored[s], 16)

            sp.wait_ge(stacks_clear, 1)
            sp.dma_start(m_dram.rearrange("g s (j n) -> (g s j) n", j=HG), m_zero[0:G * 3 * HG, :]).then_inc(m_stored, 16)
            sp.wait_ge(r_rows_ready, 1)
            for p in range(2):
                for j in range(HG):
                    sp.dma_start(q_st[p][SH:SH + 3, j, :], r_rows[0:1, :, :]).then_inc(shift_rows_loaded, 16)
            sp.wait_ge(m_stored, 16)
            sp.wait_ge(shift_rows_loaded, 16 * 2 * HG)

            def of_group(s, g):
                return part_dram[s].rearrange("g s (d j) t -> g (s d) (j t)", j=HG)[bass.ds(g, 1)]

            def load_q(g, p, done):
                q = of_group(0, g)
                for i in range(3):
                    rows = slice(3 * HD * i, 3 * HD * (i + 1))
                    qi = q[:, HD * i:HD * (i + 1), :]
                    qi = bass.AP(qi.tensor, qi.offset, [[0, 3], *qi.ap[1:]])
                    sp.dma_start(q_st[p][rows, :, :].rearrange("s j t -> s (j t)"), qi).then_inc(done, 16)
                sp.dma_start(q_st[p][SH + 3:SH + 6, :, :].rearrange("s j t -> s (j t)"),
                             m_dram[bass.ds(g, 1)].rearrange("g s n -> (g s) n")).then_inc(done, 16)

            def load_k(g, p, done):
                k = of_group(1, g)
                k = bass.AP(k.tensor, k.offset, [[0, 3], *k.ap[1:]])
                sp.dma_start(k_st[p][0:PROD, :, :].rearrange("s j t -> s (j t)"), k).then_inc(done, 16)

            sp.wait_ge(r_known, 1)
            large = sp.value_load(flag[0:1, 0:1], min_val=0, max_val=1)
            with sp.If(large > 0):
                for b in range(B):
                    for s in range(2):
                        store_parts(s, b)
                        sp.wait_ge(parts_stored[s], 16 * 3 * (b + 1))
                sp.sem_inc(ex_stored, 16)
                with sp.Fori(0, G) as g:
                    sp.wait_ge(ex_parts, g + 1)
                    load_q(g, 0, ex_loaded)
                    load_k(g, 0, ex_loaded)
                    sp.wait_ge(ex_parts, g + 2)
                    sp.dma_start(m_dram[bass.ds(g, 1)].rearrange("g s (u n) -> (g u) s n", u=HG * KT),
                                 mx_parts[:]).then_inc(ex_stored, 16)
                sp.wait_ge(ex_stored, 16 * (G + 1))
                for p in range(2):
                    load_q(p, p, stack_loaded[p])
                    load_k(p, p, stack_loaded[p])

            with sp.If(large < 1):
                store_parts(0, 0)
                sp.wait_ge(parts_stored[0], 16 * 3)
                load_q(0, 0, stack_loaded[0])
                store_parts(1, 0)
                sp.wait_ge(parts_stored[1], 16 * 3)
                load_k(0, 0, stack_loaded[0])
                load_q(1, 1, stack_loaded[1])
                load_k(1, 1, stack_loaded[1])
                for s in range(2):
                    store_parts(s, 1)
            for s in range(2):
                sp.wait_ge(parts_stored[s], 16 * 3 * B)
            with sp.Fori(1, PAIRS) as i:
                for p in range(2):
                    sp.wait_ge(scores_ready, (i - 1) * BT + (p + 1) * TILES)
                    load_q(i * 2 + p, p, stack_loaded[p])
                    load_k(i * 2 + p, p, stack_loaded[p])

            for c in range(C):
                sp.wait_ge(out_ready, c + 1)
                sp.dma_start(out_dram[:, chunk(c), :], y_out[:, chunk(c), :]).then_inc(out_stored, 16)
            sp.wait_ge(out_stored, 16 * C)

        @block.gpsimd
        def _(pool):
            nc.gpsimd.memset(ident[:], 0.0).then_inc(const_step, 1)
            nc.gpsimd.memset(minus_half[:], -0.5)
            nc.gpsimd.memset(eps[:], RMS_EPS).then_inc(const_step, 1)
            pool.wait_ge(const_step, 2)
            nc.gpsimd.affine_select(out=ident[:], in_=ident[:], compare_op=ALU.not_equal, fill=1.0, base=0,
                                    pattern=[[-1, P]], channel_multiplier=1).then_inc(consts_ready, 1)
            def inverse_std(stage, c):
                t = chunk(c)
                pool.wait_ge(stats_ready[stage], c + 1)
                nc.gpsimd.tensor_scalar(var_eps[:, t], mean_var[:, t, 1], LN_EPS, None, ALU.add).then_inc(var_ready, 1)
                pool.wait_ge(var_ready, stage * C + c + 1)
                nc.gpsimd.tensor_tensor(rstd[:, t], var_eps[:, t], minus_half[:, t], ALU.pow
                                        ).then_inc(rstd_ready[stage], 1)

            def scale_qk(c):
                for s in range(2):
                    pool.wait_ge(sum_ready, 2 * c + s + 1)
                    pool.wait_ge(r_ready, 2 * c + s + 1)
                    nc.gpsimd.tensor_tensor(qk[:, c, s, :], qk[:, c, s, :], qk_ms[:, c, s, :], ALU.mult
                                            ).then_inc(qk_scaled, 1)

            for c in range(C):
                inverse_std(0, c)
            pool.wait_ge(rows_loaded, 32)
            nc.gpsimd.tensor_scalar(b2h_row[:], b2_row[:], 0.5, None, ALU.mult).then_inc(const_step, 1)
            pool.wait_ge(const_step, 3)
            for c in range(C):
                pool.wait_ge(x_loaded[c], 16)
                nc.gpsimd.tensor_tensor(x_b[:, chunk(c), :], x_in[:, chunk(c), :],
                                        b2h_row[:].unsqueeze(1).to_broadcast([P, TC, D]), ALU.add).then_inc(xb_ready, 1)
            nc.gpsimd.memset(v_aug[:], 1.0).then_inc(ones_ready, 1)
            for p in range(2):
                nc.gpsimd.memset(q_st[p][:].bitcast(U32), 0)
                nc.gpsimd.memset(k_st[p][:].bitcast(U32), 0)
            nc.gpsimd.memset(acc_sb[:, 0, :].bitcast(U32), 0).then_inc(const_step, 1)
            nc.gpsimd.memset(acc_sb[:, 1, :].bitcast(U32), 0).then_inc(acc_copied, 1)
            for c in range(C):
                inverse_std(1, c)
                if c == 0:
                    pool.wait_ge(const_step, 4)
                    pool.wait_ge(rstd_ready[1], 1)
                    for p in range(2):
                        last = nc.gpsimd.memset(k_st[p][SH:ROWS, :, :].bitcast(U32), ONES)
                    last.then_inc(stacks_clear, 1)
                    pool.wait_ge(stacks_clear, 1)
                if c >= 2:
                    for cc in ((0, 1), (2, 3))[c - 2]:
                        scale_qk(cc)
            pool.wait_ge(v_used, C)
            def stage_v(i, p):
                nc.gpsimd.tensor_copy(v_st[p][:], v_aug[:, bass.ds(i * 2 + p, 1)].rearrange("p g k v -> p (g k) v")
                                      ).then_inc(v_staged[p], 1)

            for p in range(2):
                stage_v(0, p)
            with pool.Fori(1, PAIRS) as i:
                for p in range(2):
                    pool.wait_ge(pv_done, (i - 1) * (2 * STEPS) + (p + 1) * STEPS + PB // 2)
                    stage_v(i, p)

            for c in range(C):
                nc.gpsimd.tensor_tensor(x_b[:, chunk(c), :], x_1[:, chunk(c), :],
                                        bo_row[:].unsqueeze(1).to_broadcast([P, TC, D]), ALU.add).then_inc(xb2_ready, 1)

            for c in range(C):
                inverse_std(2, c)
            for c in range(C):
                nc.gpsimd.tensor_tensor(x_b[:, chunk(c), :], x_2[:, chunk(c), :],
                                        b2h_row[:].unsqueeze(1).to_broadcast([P, TC, D]), ALU.add).then_inc(xb3_ready, 1)

        @block.scalar
        def _(act):
            act.dma_start(vec_rows[:], b1.rearrange("(m p) -> m p", p=P)).then_inc(vec_loaded, 16)
            act.dma_start(wq_sb[:], Wq).then_inc(attn_w_loaded, 16)
            act.dma_start(wk_sb[:], Wk).then_inc(attn_w_loaded, 16)
            for row, vec in enumerate((bq[0:D], bk)):
                act.dma_start(qk_rows[row:row + 1, :], vec.unsqueeze(0)).then_inc(qk_rows_loaded, 16)
            for row, vec in ((2, qn_w), (3, kn_w)):
                act.dma_start(qk_rows[row:row + 1, :].rearrange("o (h d) -> o h d", d=HD), per_head(vec)
                              ).then_inc(qk_rows_loaded, 16)
            act.dma_start(wv_sb[:], Wv).then_inc(attn_w_loaded, 16)
            act.dma_start(qn_row[:], qn_w.partition_broadcast(P)).then_inc(r_w_loaded, 16)
            act.dma_start(kn_row[:], kn_w.partition_broadcast(P)).then_inc(r_w_loaded, 16)

            def copy_turned(n, dst, c):
                act.wait_ge(turned, n + 1)
                nc.scalar.copy(dst[:, cols(c)], t_bank(n)).then_inc(turned_copied, 1)

            def gelu(f, c):
                if c >= 2:
                    act.wait_ge(y_psum[f], c - 1)
                for m in range(M):
                    act.wait_ge(h_psum[f], M * c + m + 1)
                    nc.scalar.activation(hT[:, c % 2, m, :], h_bank(m), ACT.Gelu,
                                         bias=b1_col[:, m:m + 1]).then_inc(h_ready[f], 1)

            def qk_sums(c):
                for s, b_col in ((0, bq_col), (1, bk_col)):
                    act.wait_ge(qk_psum, 2 * c + s + 1)
                    if c >= 1:
                        act.wait_ge(ms_psum, 2 * c - 1 + s)
                    nc.scalar.activation(qk_sq[:, s, :], ps[:, Q_BANK + s, :], ACT.Square, bias=b_col)
                    nc.scalar.activation(qk[:, c, s, :], ps[:, Q_BANK + s, :], ACT.Identity,
                                         bias=qk_bw_col[:, s:s + 1], scale=qk_w_col[:, s:s + 1]).then_inc(sum_ready, 1)

            def copy_ms(c):
                for s in range(2):
                    act.wait_ge(ms_psum, 2 * c + s + 1)
                    nc.scalar.copy(qk_ms[:, c, s, :], ps[:, Q_BANK + s, :]).then_inc(ms_ready, 1)

            def inverse_rms(c):
                for s in range(2):
                    if c == 0:
                        act.wait_ge(ms_ready, s + 1)
                        ms = qk_ms[:, c, s, :]
                    else:
                        act.wait_ge(ms_psum, 2 * c + s + 1)
                        ms = ps[:, Q_BANK + s, :]
                    nc.scalar.activation(qk_ms[:, c, s, :], ms, ACT.Ln, bias=eps[:, 0:1]).then_inc(ln_ready, 1)
                for s in range(2):
                    act.wait_ge(ln_ready, 2 * c + s + 1)
                    nc.scalar.activation(qk_ms[:, c, s, :], qk_ms[:, c, s, :], ACT.Exp, scale=-0.5
                                         ).then_inc(r_ready, 1)

            nc.scalar.preload_act_table(ACT.Gelu)
            copy_turned(0, x_nT, 0)
            copy_turned(1, x_nT, 1)
            act.wait_ge(vec_ready, 1)
            gelu(0, 0)
            copy_turned(2, x_nT, 2)
            gelu(0, 1)
            copy_turned(3, x_nT, 0)
            gelu(0, 2)
            copy_turned(4, x_nT, 3)
            act.wait_ge(vec_ready, 3)
            qk_sums(0)
            copy_turned(5, x_nT, 1)
            gelu(0, 3)
            copy_ms(0)
            act.wait_ge(consts_ready, 1)
            nc.scalar.preload_act_table_set("natural_log_exp_and_others")
            inverse_rms(0)
            qk_sums(1)
            inverse_rms(1)
            copy_turned(6, x_nT, 2)
            qk_sums(2)
            copy_turned(7, x_nT, 3)
            inverse_rms(2)
            qk_sums(3)
            inverse_rms(3)
            act.wait_ge(gate_sum, 1)
            nc.scalar.activation(gate[:], gate[:], ACT.Exp, scale=-1.0).then_inc(gate_exp, 1)

            act.wait_ge(v_used, C)
            act.wait_ge(gate_sum, 1)
            act.sem_inc(probs_ready, FREE3)

            def exp_tiles(i, first, last):
                for n in range(first, last):
                    act.wait_ge(scores_ready, i * BT + n + 1)
                    act.wait_ge(pv_done, i * (BT // 2) + n // 2 + 1)
                    b = SBUF_OF[n]
                    nc.scalar.activation(probs[:, n % PB, :], ps[:, 2 * b:2 * b + 2, :].rearrange("p b n -> p (b n)"),
                                         ACT.Exp).then_inc(probs_ready, 1)

            with act.Fori(0, PAIRS) as i:
                exp_tiles(i, 0, BT)

            for c in range(C):
                copy_turned(8 + c, oT, c)
            nc.scalar.preload_act_table(ACT.Gelu)
            copy_turned(12, x_nT, 0)
            copy_turned(13, x_nT, 1)
            gelu(1, 0)
            copy_turned(14, x_nT, 2)
            gelu(1, 1)
            gelu(1, 2)
            copy_turned(15, x_nT, 3)
            gelu(1, 3)

        @block.vector
        def _(dve):
            count = [0]

            def done(ins):
                count[0] += 1
                ins.then_inc(dve_step, 1)
                dve.wait_ge(dve_step, count[0])

            def token_stats(stage, src, c):
                for t in range(c * TC, (c + 1) * TC):
                    last = nc.vector.bn_stats(stats[:, t, :], src[:, t, :])
                done(last)
                for t in range(c * TC, (c + 1) * TC):
                    last = nc.vector.bn_aggr(mean_var[:, t, :], stats[:, t, :])
                last.then_inc(stats_ready[stage], 1)

            def normalise(stage, src, c):
                dve.wait_ge(rstd_ready[stage], c + 1)
                dve.wait_ge(stats_ready[stage], c + 1)
                for t in range(c * TC, (c + 1) * TC):
                    last = nc.vector.tensor_scalar(x_n[:, t, :], src[:, t, :], mean_var[:, t, 0:1], rstd[:, t:t + 1],
                                                   ALU.subtract, ALU.mult)
                last.then_inc(xn_ready[stage], 1)

            dve.sem_inc(o_ready, FREE2)
            for c in range(C):
                if c == 2:
                    dve.wait_ge(vec_psum, 1)
                    nc.vector.tensor_copy(vec_cols[:, 0:M], ps[:, 7, 0:M]).then_inc(vec_ready, 1)
                dve.wait_ge(x_loaded[c], 16)
                token_stats(0, x_in, c)
                if c >= 1:
                    normalise(0, x_in, c - 1)
            normalise(0, x_in, C - 1)

            dve.wait_ge(r_w_loaded, 16 * 2)
            dve.wait_ge(qk_rows_loaded, 16 * 4)
            nc.vector.tensor_copy(qk_rows_p[:].rearrange("p (g d j) -> p g d j", d=HD, j=HG),
                                  qk_rows[:].rearrange("p (g j d) -> p g d j", d=HD, j=HG)).then_inc(qk_rows_ready, 1)
            dve.wait_ge(attn_w_loaded, 16 * 5)
            for s, w in ((0, wq_sb[:, 0:D]), (1, wk_sb[:])):
                last = nc.vector.tensor_copy(wqk_p[:, s, :].rearrange("p (g d j) -> p g d j", d=HD, j=HG),
                                             w.rearrange("p (g j d) -> p g d j", d=HD, j=HG))
            last.then_inc(qk_w_ready, 1)
            dve.wait_ge(consts_ready, 1)
            done(nc.vector.reduce_sum(head_sum[:].rearrange("p (g j) -> p g j", j=HG),
                                      ident[:].rearrange("p (g d j) -> p g j d", d=HD, j=HG), AX_X))
            nc.vector.tensor_scalar(head_mean[:].rearrange("p (g d j) -> p g d j", d=HD, j=HG),
                                    head_sum[:].rearrange("p (g j) -> p g j", j=HG).unsqueeze(2)
                                    .to_broadcast([P, GB, HD, HG]), 1.0 / HD, None, ALU.mult).then_inc(consts_ready, 1)
            dve.wait_ge(vec_psum, 2)
            nc.vector.tensor_copy(vec_cols[:, M:M + 4], ps[:, 7, M:M + 4]).then_inc(vec_ready, 1)
            dve.wait_ge(vec_ready, 2)
            nc.vector.tensor_copy(qk_w_col[:, 1:2], kn_col)
            done(nc.vector.tensor_scalar(qk_w_col[:, 0:1], qn_col, float(HD) ** -0.5, None, ALU.mult))
            nc.vector.tensor_tensor(qk_bw_col[:], vec_cols[:, M:M + 2], qk_w_col[:], ALU.mult).then_inc(vec_ready, 1)
            done(nc.vector.tensor_tensor(r_w[:, 0, :], qn_row[:], kn_row[:], ALU.mult))
            done(nc.vector.tensor_scalar(r_w[:, 1, :], r_w[:, 0, :], -1.0, None, ALU.mult))
            done(nc.vector.tensor_tensor(r_w[:, 2, :], r_w[:, 0, :], r_w[:, 1, :], ALU.max))
            done(nc.vector.reduce_max(r_col[:, 0:1], r_w[:, 2, :], AX_X))
            done(nc.vector.tensor_scalar(r_col[:, 1:2], r_col[:, 0:1], -float(HD) ** 0.5, None, ALU.mult))
            nc.vector.tensor_scalar(flag[:], r_col[:, 1:2], -SHIFT_SAFE, None, ALU.is_lt).then_inc(r_known, 1)
            done(nc.vector.tensor_copy(r_bf[:, 0:1], r_col[:, 1:2]))
            done(nc.vector.tensor_tensor(r_col[:, 2:3], r_col[:, 1:2], r_bf[:, 0:1], ALU.subtract))
            done(nc.vector.tensor_copy(r_bf[:, 1:2], r_col[:, 2:3]))
            done(nc.vector.tensor_tensor(r_col[:, 3:4], r_col[:, 2:3], r_bf[:, 1:2], ALU.subtract))
            for s, part in enumerate((r_bf[0:1, 0:1], r_bf[0:1, 1:2], r_col[0:1, 3:4])):
                last = nc.vector.tensor_copy(r_rows[0:1, s, :], part.to_broadcast([1, N]))
            last.then_inc(r_rows_ready, 1)

            def ffn_sum(c):
                dve.wait_ge(xb_ready, c + 1)
                dve.wait_ge(y_psum[0], c + 1)
                ins = nc.vector.scalar_tensor_tensor(
                    out=x_1[:, chunk(c), :].rearrange("p t d -> p (t d)"), in0=ps[:, Y_BANK, :], scalar=0.5,
                    in1=x_b[:, chunk(c), :].rearrange("p t d -> p (t d)"), op0=ALU.mult, op1=ALU.add)
                ins.then_inc(y_used[0], 1)
                dve.wait_ge(y_used[0], c + 1)
                token_stats(1, x_1, c)

            def v_sum(c):
                dve.wait_ge(v_psum, c + 1)
                for tl in range(TC):
                    b, kt = divmod(c * TC + tl, KT)
                    last = nc.vector.tensor_tensor(
                        v_aug[:, b * GB:(b + 1) * GB, kt, :].rearrange("p g (j v) -> p g j v", v=VW)[:, :, :, 0:HD],
                        ps[:, V_BANK, tl * D:(tl + 1) * D].rearrange("p (g j d) -> p g j d", j=HG, d=HD),
                        bv_row[:].rearrange("p (g j d) -> p g j d", j=HG, d=HD), ALU.add)
                last.then_inc(v_used, 1)

            def split(s, c):
                b = c * 512 // N
                if b > 0:
                    dve.wait_ge(parts_stored[s], 16 * 3 * b)
                at = slice(c * 512 % N, c * 512 % N + 512)
                dve.wait_ge(qk_scaled, 2 * c + s + 1)
                x = qk[:, c, s, :]
                n = 3 * (4 * b + 2 * s + c % 2)
                nc.vector.tensor_copy(parts[:, s, 0, at], x).then_inc(parts_ready, 1)
                dve.wait_ge(parts_ready, n + 1)
                done(nc.vector.tensor_tensor(x, x, parts[:, s, 0, at], ALU.subtract))
                nc.vector.tensor_copy(parts[:, s, 1, at], x).then_inc(parts_ready, 1)
                dve.wait_ge(parts_ready, n + 2)
                nc.vector.tensor_tensor(parts[:, s, 2, at], x, parts[:, s, 1, at],
                                        ALU.subtract).then_inc(parts_ready, 1)

            ffn_sum(0)
            normalise(1, x_1, 0)
            ffn_sum(1)
            normalise(1, x_1, 1)
            dve.wait_ge(attn_w_loaded, 16 * 5)
            dve.wait_ge(ones_ready, 1)
            v_sum(0)
            ffn_sum(2)
            normalise(1, x_1, 2)
            split(0, 0)
            v_sum(1)
            ffn_sum(3)
            split(0, 1)
            normalise(1, x_1, 3)
            v_sum(2)
            split(1, 0)
            split(1, 1)
            v_sum(3)
            dve.wait_ge(gate_psum, 2)
            nc.vector.tensor_tensor(gate[:], ps[:, GATE_BANK, 0:T * H].rearrange("p (t h) -> p t h", h=H),
                                    bg_row[:].unsqueeze(1).to_broadcast([P, T, H]), ALU.add).then_inc(gate_sum, 1)
            split(0, 2)
            split(0, 3)
            split(1, 2)
            split(1, 3)
            dve.wait_ge(gate_exp, 1)
            done(nc.vector.tensor_scalar(gate[:], gate[:], 1.0, None, ALU.add))
            for b in range(B):
                last = nc.vector.reciprocal(
                    sig[:, b * GB:(b + 1) * GB, :, :],
                    gate[:, b * KT:(b + 1) * KT, :].rearrange("p t (g j) -> p g t j", j=HG))
            last.then_inc(sig_ready, 1)

            dve.wait_ge(r_known, 1)
            large = dve.value_load(flag[0:1, 0:1], min_val=0, max_val=1)
            U = HG * KT
            with dve.If(large > 0):
                dve.sem_inc(ex_parts, 1)
                with dve.Fori(0, G) as g:
                    for u in range(U):
                        dve.wait_ge(ex_scores, g * U + u + 1)
                        nc.vector.reduce_max(mx[:, u:u + 1], ps[:, 2 * (u % 2):2 * (u % 2) + 2, :]
                                             .rearrange("p b n -> p (b n)"), AX_X).then_inc(ex_max, 1)
                    dve.wait_ge(ex_mT, g + 1)
                    nc.vector.tensor_scalar(mx_n[:], ps[0:U, 4, 0:P], -1.0, None, ALU.mult).then_inc(ex_step, 1)
                    dve.wait_ge(ex_step, g * 4 + 1)
                    dve.wait_ge(ex_stored, g * 16 + 16)
                    nc.vector.tensor_copy(mx_parts[:, 0, :], mx_n[:]).then_inc(ex_step, 1)
                    dve.wait_ge(ex_step, g * 4 + 2)
                    nc.vector.tensor_tensor(mx_r[:], mx_n[:], mx_parts[:, 0, :], ALU.subtract).then_inc(ex_step, 1)
                    dve.wait_ge(ex_step, g * 4 + 3)
                    nc.vector.tensor_copy(mx_parts[:, 1, :], mx_r[:]).then_inc(ex_step, 1)
                    dve.wait_ge(ex_step, g * 4 + 4)
                    nc.vector.tensor_tensor(mx_parts[:, 2, :], mx_r[:], mx_parts[:, 1, :],
                                            ALU.subtract).then_inc(ex_parts, 1)

            dve.wait_ge(sig_ready, 1)
            def finish(b, i, k):
                half = k % 2
                bank = ACC + half
                item = (b * (GB // 2) + i) * 4 + k
                g = b * GB + i * 2 + k // 2
                heads = bass.ds((i * 2 + k // 2) * (HG * HD), HG * HD)
                dve.wait_ge(pv_done, item * KT + KT + PB // 2)
                nc.vector.tensor_copy(acc_sb[:, half, :], ps[:, bank, :]).then_inc(acc_copied, 1)
                dve.wait_ge(accT_psum, (item + 1) * 4 + 4)
                rows = ps[:, bank, :].rearrange("p (t j v) -> p t j v", j=HG, v=32)
                nc.vector.reciprocal(r_den[:], rows[:, :, :, HD]).then_inc(norm_step, 1)
                dve.wait_ge(norm_step, item * 2 + 1)
                nc.vector.tensor_tensor(fac[:], r_den[:], sig[:, bass.ds(g, 1), 4 * half:4 * half + 4, :]
                                        .rearrange("p g t j -> p (g t) j"), ALU.mult).then_inc(norm_step, 1)
                dve.wait_ge(norm_step, item * 2 + 2)
                nc.vector.tensor_tensor(
                    o_nat[:, bass.ds(b * KT + 4 * half, 4), heads].rearrange("p t (j d) -> p t j d", d=HD),
                    rows[:, :, :, 0:HD], fac[:].unsqueeze(3).to_broadcast([P, 4, HG, HD]),
                    ALU.mult).then_inc(o_ready, 1)

            with dve.Fori(0, B) as b:
                with dve.Fori(0, GB // 2) as i:
                    for k in range(4):
                        finish(b, i, k)

            def o_sum(c):
                dve.wait_ge(xb2_ready, c + 1)
                dve.wait_ge(o_psum, c + 1)
                nc.vector.tensor_tensor(x_2[:, chunk(c), :].rearrange("p t d -> p (t d)"), ps[:, V_BANK, :],
                                        x_b[:, chunk(c), :].rearrange("p t d -> p (t d)"), ALU.add).then_inc(o_used, 1)
                dve.wait_ge(o_used, c + 1)
                token_stats(2, x_2, c)

            o_sum(0)
            for c in range(1, C):
                o_sum(c)
                normalise(2, x_2, c - 1)
            normalise(2, x_2, C - 1)
            for c in range(C):
                dve.wait_ge(xb3_ready, c + 1)
                dve.wait_ge(y_psum[1], c + 1)
                nc.vector.scalar_tensor_tensor(
                    out=y_out[:, chunk(c), :].rearrange("p t d -> p (t d)"), in0=ps[:, Y_BANK, :], scalar=0.5,
                    in1=x_b[:, chunk(c), :].rearrange("p t d -> p (t d)"), op0=ALU.mult, op1=ALU.add
                ).then_inc(out_ready, 1)

        @block.tensor
        def _(pe):
            def turn_chunk(n, src, c):
                if n >= 2:
                    pe.wait_ge(turned_copied, n - 1)
                for tl in range(TC):
                    last = nc.tensor.transpose(t_bank(n)[:, tl * P:(tl + 1) * P], src[:, c * TC + tl, :], ident[:])
                last.then_inc(turned, 1)

            def turn_xn(n, stage, c):
                pe.wait_ge(xn_ready[stage], c + 1)
                turn_chunk(n, x_n, c)

            def ffn_in(f, n, c):
                pe.wait_ge(turned_copied, n + 1)
                for m in range(M):
                    if M * c + m >= 2:
                        pe.wait_ge(h_ready[f], M * c + m - 1)
                    nc.tensor.matmul(h_bank(m), w1_sb[:, m * P:(m + 1) * P], x_nT[:, cols(c)],
                                     start=True, stop=True).then_inc(h_psum[f], 1)

            def ffn_out(f, c, used):
                pe.wait_ge(h_ready[f], M * (c + 1))
                if c >= 1:
                    pe.wait_ge(used, c)
                for tl in range(TC):
                    for m in range(M):
                        last = nc.tensor.matmul(ps[:, Y_BANK, tl * D:(tl + 1) * D],
                                                hT[:, c % 2, m, tl * P:(tl + 1) * P],
                                                w2_sb[:, m, :], start=(m == 0), stop=(m == M - 1))
                last.then_inc(y_psum[f], 1)

            def qkv(n, c):
                pe.wait_ge(turned_copied, n + 1)
                for s, w in ((0, wqk_p[:, 0, :]), (1, wqk_p[:, 1, :])):
                    if c == 1:
                        pe.wait_ge(ms_ready, s + 1)
                    if c >= 2:
                        pe.wait_ge(ln_ready, 2 * c - 1 + s)
                    nc.tensor.matmul(ps[:, Q_BANK + s, :], w, x_nT[:, cols(c)], start=True, stop=True
                                     ).then_inc(qk_psum, 1)
                if c >= 1:
                    pe.wait_ge(v_used, c)
                for tl in range(TC):
                    t = c * TC + tl
                    last = nc.tensor.matmul(ps[:, V_BANK, tl * D:(tl + 1) * D], x_nT[:, t * P:(t + 1) * P], wv_sb[:],
                                            start=True, stop=True)
                last.then_inc(v_psum, 1)

            def mean_squares(c):
                for s in range(2):
                    pe.wait_ge(sum_ready, 2 * c + s + 1)
                    nc.tensor.matmul(ps[:, Q_BANK + s, :], head_mean[:], qk_sq[:, s, :], start=True, stop=True
                                     ).then_inc(ms_psum, 1)

            def gates(first, last):
                for t in range(first, last):
                    ins = nc.tensor.matmul(ps[:, GATE_BANK, t * H:(t + 1) * H], x_nT[:, t * P:(t + 1) * P],
                                           wq_sb[:, D:D + H], start=True, stop=True)
                ins.then_inc(gate_psum, 1)

            pe.wait_ge(consts_ready, 1)
            turn_xn(0, 0, 0)
            pe.wait_ge(vec_loaded, 16)
            nc.tensor.transpose(ps[:, 7, 0:M], vec_rows[:], ident[0:M, 0:M]).then_inc(vec_psum, 1)
            turn_xn(1, 0, 1)
            pe.wait_ge(w1_loaded, 16)
            ffn_in(0, 0, 0)
            turn_xn(2, 0, 2)
            pe.wait_ge(qk_rows_ready, 1)
            pe.wait_ge(vec_ready, 1)
            nc.tensor.transpose(ps[:, 7, M:M + 4], qk_rows_p[:], ident[0:4, 0:4]).then_inc(vec_psum, 1)
            ffn_in(0, 1, 1)
            pe.wait_ge(w2_loaded, 16)
            ffn_out(0, 0, y_used[0])
            ffn_out(0, 1, y_used[0])
            turn_xn(3, 1, 0)
            ffn_in(0, 2, 2)
            turn_xn(4, 0, 3)
            pe.wait_ge(attn_w_loaded, 16 * 5)
            pe.wait_ge(qk_w_ready, 1)
            qkv(3, 0)
            turn_xn(5, 1, 1)
            ffn_in(0, 4, 3)
            pe.wait_ge(consts_ready, 2)
            mean_squares(0)
            ffn_out(0, 2, y_used[0])
            qkv(5, 1)
            mean_squares(1)
            ffn_out(0, 3, y_used[0])
            turn_xn(6, 1, 2)
            qkv(6, 2)
            pe.wait_ge(h_ready[0], M * C)
            gates(0, 12)
            turn_xn(7, 1, 3)
            mean_squares(2)
            qkv(7, 3)
            gates(12, T)
            mean_squares(3)

            pe.wait_ge(y_used[0], C)
            pe.wait_ge(v_used, C)
            pe.wait_ge(turned_copied, 2 * C)
            pe.wait_ge(ln_ready, 2 * C)
            pe.wait_ge(gate_sum, 1)

            pe.wait_ge(r_known, 1)
            large = pe.value_load(flag[0:1, 0:1], min_val=0, max_val=1)
            U = HG * KT
            with pe.If(large > 0):
                pe.sem_inc(ex_max, 2)
                with pe.Fori(0, G) as g:
                    pe.wait_ge(ex_loaded, g * (16 * LOADS) + 16 * LOADS)
                    for u in range(U):
                        j, qt = divmod(u, KT)
                        pe.wait_ge(ex_max, g * U + u + 1)
                        for h in range(2):
                            last = nc.tensor.matmul(ps[:, 2 * (u % 2) + h, :], q_st[0][0:ROWS, j, qt * P:(qt + 1) * P],
                                                    k_st[0][0:ROWS, j, h * 512:(h + 1) * 512], start=True, stop=True)
                        last.then_inc(ex_scores, 1)
                    pe.wait_ge(ex_max, g * U + U + 2)
                    nc.tensor.transpose(ps[0:U, 4, 0:P], mx[:], ident[:]).then_inc(ex_mT, 1)
                pe.wait_ge(ex_parts, G + 1)

            pe.sem_inc(pv_done, PB // 2)

            def scores(i, n, wait=True):
                p, m = divmod(n % BT, TILES)
                step, jj = divmod(m, 2)
                half, kt = divmod(step, KT)
                if m == 0:
                    pe.wait_ge(stack_loaded[p], (i + n // BT) * (16 * LOADS) + 16 * LOADS)
                pe.wait_ge(probs_ready, i * BT + (n - n % BT) + PREV[n % BT] + 1 + FREE3)
                for u in range(2):
                    j = 2 * jj + u
                    last = nc.tensor.matmul(ps[:, 2 * SBUF_OF[n % BT] + u, :],
                                            k_st[p][0:ROWS, j, kt * P:(kt + 1) * P],
                                            q_st[p][0:ROWS, j, half * 512:(half + 1) * 512], start=True, stop=True)
                last.then_inc(scores_ready, 1)

            def weighted(i, s):
                p, step = divmod(s, STEPS)
                half, kt = divmod(step, KT)
                if step == 0:
                    pe.wait_ge(v_staged[p], i + 1)
                if kt == 0:
                    pe.wait_ge(o_ready, i * 4 + 2 * p + half + 1)
                pe.wait_ge(probs_ready, i * BT + 2 * s + 2 + FREE3)
                for j in range(HG):
                    last = nc.tensor.matmul(ps[32 * j:32 * j + VW, ACC + half, :],
                                            v_st[p][:, kt, j * VW:(j + 1) * VW],
                                            probs[:, (2 * s + j // 2) % PB, (j % 2) * 512:(j % 2 + 1) * 512],
                                            start=(kt == 0), stop=(kt == KT - 1))
                last.then_inc(pv_done, 1)

            def turn(i, k, t):
                half = k % 2
                pe.wait_ge(acc_copied, i * 4 + k + 2)
                nc.tensor.transpose(ps[:, ACC + half, t * P:(t + 1) * P],
                                    acc_sb[:, half, t * P:(t + 1) * P], ident[:]).then_inc(accT_psum, 1)

            def iteration(i, final):
                for s in range(2 * STEPS):
                    if not (final and 2 * s + 4 >= BT):
                        scores(i, 2 * s + 4)
                    weighted(i, s)
                    if not (final and 2 * s + 5 >= BT):
                        scores(i, 2 * s + 5)
                    if 1 <= s % KT <= 4:
                        turn(i, s // KT - 1, s % KT - 1)

            for n in range(4):
                scores(0, n)
            with pe.Fori(0, PAIRS - 1) as i:
                iteration(i, False)
            iteration(PAIRS - 1, True)
            for t in range(4):
                turn(PAIRS - 1, 3, t)

            pe.wait_ge(wo_loaded, 16)
            pe.wait_ge(o_ready, 2 * G + FREE2)
            def project(c):
                pe.wait_ge(turned_copied, 2 * C + c + 1)
                if c >= 1:
                    pe.wait_ge(o_used, c)
                for tl in range(TC):
                    t = c * TC + tl
                    last = nc.tensor.matmul(ps[:, V_BANK, tl * D:(tl + 1) * D], oT[:, t * P:(t + 1) * P], wo_sb[:],
                                            start=True, stop=True)
                last.then_inc(o_psum, 1)

            turn_chunk(8, o_nat, 0)
            turn_chunk(9, o_nat, 1)
            project(0)
            turn_chunk(10, o_nat, 2)
            project(1)
            turn_chunk(11, o_nat, 3)
            project(2)
            turn_xn(12, 2, 0)
            project(3)
            turn_xn(13, 2, 1)
            ffn_in(1, 12, 0)
            turn_xn(14, 2, 2)
            ffn_in(1, 13, 1)
            ffn_out(1, 0, out_ready)
            ffn_in(1, 14, 2)
            turn_xn(15, 2, 3)
            ffn_out(1, 1, out_ready)
            ffn_in(1, 15, 3)
            ffn_out(1, 2, out_ready)
            ffn_out(1, 3, out_ready)


_INS = ["L0_attn_x", "L0_attn_Wq", "L0_attn_bq", "L0_attn_Wk", "L0_attn_bk", "L0_attn_Wv", "L0_attn_bv",
        "L0_attn_Wo", "L0_attn_bo", "L0_attn_qn_w", "L0_attn_kn_w", "L0_ffn_w1", "L0_ffn_b1", "L0_ffn_w2",
        "L0_ffn_b2"]
_OUTS = [((2, 1024, 128), "float32")]


def kernel(**inputs):
    import numpy as _np
    import concourse.bacc as _bacc
    from concourse import mybir as _mybir
    from concourse.bass_utils import run_bass_kernel_spmd as _run

    nc = _bacc.Bacc("TRN2", target_bir_lowering=False, num_devices=1)
    arrays, args = {}, []
    for name in _INS:
        a = _np.ascontiguousarray(inputs[name])
        arrays[f"in_{name}"] = a
        args.append(nc.dram_tensor(f"in_{name}", a.shape, _mybir.dt.from_np(a.dtype), kind="ExternalInput").ap())
    for i, (shape, dtype) in enumerate(_OUTS):
        dt = _mybir.dt.from_np(_np.dtype(dtype))
        args.append(nc.dram_tensor(f"out_{i}", shape, dt, kind="ExternalOutput").ap())
    macaron_kernel(nc, *args)
    r = _run(nc, [arrays], core_ids=[0])
    got = tuple(r.results[0][f"out_{i}"] for i in range(len(_OUTS)))
    return got[0]
```

```python
from contextlib import ExitStack

import numpy as np

import concourse.bass as bass
from concourse import mybir

F32 = mybir.dt.float32
BF16 = mybir.dt.bfloat16
I32 = mybir.dt.int32
U32 = mybir.dt.uint32
ALU = mybir.AluOpType
ACT = mybir.ActivationFunctionType
AX_X = mybir.AxisListType.X

LN_EPS = 1e-5
RMS_EPS = 1e-6
ONES = 0x3F803F80
SHIFT_SAFE = 30.0


def macaron_kernel(nc, x, Wq, bq, Wk, bk, Wv, bv, Wo, bo, qn_w, kn_w, w1, b1, w2, b2, out):
    P = 128
    B, N, D = x.shape
    H = Wq.shape[1] - D
    HD = D // H
    F = w1.shape[1]
    T = B * N // P
    C = B * N // 512
    TC = T // C
    M = F // P
    assert (P, D, HD, TC, T, M) == (128, 128, 8, 4, 16, 4)
    HG = 4
    G = B * H // HG
    GB = G // B
    KT = N // P
    VW = HD + 1
    PAIRS = G // 2
    PROD = 9 * HD
    SH = 96
    ROWS = SH + 6
    STEPS = 2 * KT
    TILES = 2 * STEPS
    BT = 2 * TILES
    SBUF_OF = [0, 1, 2] * ((BT - 4) // 3) + [0, 1, 0, 2]
    PREV = [max([m for m in range(-BT, n) if SBUF_OF[m % BT] == SBUF_OF[n]]) for n in range(BT)]
    FREE3 = 3
    FREE2 = 2
    PB = 8
    ACC = 6
    LOADS = 5

    with ExitStack() as ctx:
        def sb(name, shape, dt=F32):
            return ctx.enter_context(nc.sbuf_tensor(name, shape, dt))

        def sem(name):
            return ctx.enter_context(nc.semaphore(name))

        ps = ctx.enter_context(nc.psum_tensor("ps", [P, 8, 512], F32))

        w1_sb = sb("w1_sb", [P, F])
        w2_sb = sb("w2_sb", [P, M, D])
        wq_sb = sb("wq_sb", [P, D + H])
        wk_sb = sb("wk_sb", [P, D])
        wv_sb = sb("wv_sb", [P, D])
        wo_sb = sb("wo_sb", [P, D])
        vec_rows = sb("vec_rows", [M, P])
        qk_rows = sb("qk_rows", [4, P])
        qk_rows_p = sb("qk_rows_p", [4, P])
        wqk_p = sb("wqk_p", [P, 2, D])
        head_sum = sb("head_sum", [P, H])
        vec_cols = sb("vec_cols", [P, M + 4])
        b1_col = vec_cols[:, 0:M]
        bq_col, bk_col, qn_col, kn_col = (vec_cols[:, M + n:M + n + 1] for n in range(4))
        qk_w_col = sb("qk_w_col", [P, 2])
        qk_bw_col = sb("qk_bw_col", [P, 2])
        b2_row = sb("b2_row", [P, D])
        b2h_row = sb("b2h_row", [P, D])
        bo_row = sb("bo_row", [P, D])
        bv_row = sb("bv_row", [P, D])
        bg_row = sb("bg_row", [P, H])
        qn_row = sb("qn_row", [P, HD])
        kn_row = sb("kn_row", [P, HD])
        ident = sb("ident", [P, P])
        head_mean = sb("head_mean", [P, P])
        eps = sb("eps", [P, 1])
        x_in = sb("x_in", [P, T, D])
        x_b = sb("x_b", [P, T, D])
        x_1 = sb("x_1", [P, T, D])
        x_2 = sb("x_2", [P, T, D])
        y_out = x_in
        x_n = sb("x_n", [P, T, D])
        stats = sb("stats", [P, T, 6])
        mean_var = sb("mean_var", [P, T, 2])
        var_eps = sb("var_eps", [P, T])
        minus_half = sb("minus_half", [P, T])
        rstd = sb("rstd", [P, T])
        x_nT = sb("x_nT", [P, T * P])
        oT = x_nT
        qk = sb("qk", [P, C, 2, 512])
        qk_sq = sb("qk_sq", [P, 2, 512])
        qk_ms = sb("qk_ms", [P, C, 2, 512])
        parts = sb("parts", [P, 2, 3, N], BF16)
        v_aug = sb("v_aug", [P, G, KT, HG * VW])
        gate = sb("gate", [P, T, H])
        sig = sb("sig", [P, G, KT, HG])
        r_w = sb("r_w", [P, 4, HD])
        r_col = sb("r_col", [P, 8])
        r_bf = sb("r_bf", [P, 2], BF16)
        r_rows = sb("r_rows", [P, 3, N], BF16)
        flag = sb("flag", [P, 1], I32)
        q_st = [sb(f"q_st{p}", [P, HG, N], BF16) for p in range(2)]
        k_st = [sb(f"k_st{p}", [P, HG, N], BF16) for p in range(2)]
        v_st = [sb(f"v_st{p}", [P, KT, HG * VW]) for p in range(2)]
        probs = sb("probs", [P, PB, 1024])
        hT = probs[:].rearrange("p (c m) (h n) -> p c (m h) n", c=C, h=2)
        acc_sb = sb("acc_sb", [P, 2, 512])
        r_den = sb("r_den", [P, 4, HG])
        fac = sb("fac", [P, 4, HG])
        o_nat = sb("o_nat", [P, T, D])
        mx = sb("mx", [P, HG * KT])
        mx_n = sb("mx_n", [HG * KT, P])
        mx_r = sb("mx_r", [HG * KT, P])
        mx_parts = sb("mx_parts", [HG * KT, 3, P], BF16)
        m_zero = acc_sb[:, 0, :].bitcast(BF16)
        m_ones = acc_sb[:, 1, :].bitcast(BF16)

        part_dram = [nc.dram_tensor(f"part_dram{s}", [G, 3, HD * HG, N], BF16, kind="Internal").ap() for s in range(2)]
        m_dram = nc.dram_tensor("m_dram", [G, 3, HG * N], BF16, kind="Internal").ap()

        x_loaded = [sem(f"x_loaded{c}") for c in range(C)]
        w1_loaded = sem("w1_loaded")
        w2_loaded = sem("w2_loaded")
        vec_loaded = sem("vec_loaded")
        vec_psum = sem("vec_psum")
        vec_ready = sem("vec_ready")
        qk_rows_loaded = sem("qk_rows_loaded")
        qk_rows_ready = sem("qk_rows_ready")
        qk_w_ready = sem("qk_w_ready")
        attn_w_loaded = sem("attn_w_loaded")
        rows_loaded = sem("rows_loaded")
        r_w_loaded = sem("r_w_loaded")
        wo_loaded = sem("wo_loaded")
        const_step = sem("const_step")
        consts_ready = sem("consts_ready")
        xb_ready = sem("xb_ready")
        xb2_ready = sem("xb2_ready")
        xb3_ready = sem("xb3_ready")
        stats_ready = [sem(f"stats_ready{k}") for k in range(3)]
        var_ready = sem("var_ready")
        rstd_ready = [sem(f"rstd_ready{k}") for k in range(3)]
        xn_ready = [sem(f"xn_ready{k}") for k in range(3)]
        turned = sem("turned")
        turned_copied = sem("turned_copied")
        h_psum = [sem(f"h_psum{k}") for k in range(2)]
        h_ready = [sem(f"h_ready{k}") for k in range(2)]
        y_psum = [sem(f"y_psum{k}") for k in range(2)]
        y_used = [sem(f"y_used{k}") for k in range(2)]
        dve_step = sem("dve_step")
        qk_psum = sem("qk_psum")
        v_psum = sem("v_psum")
        v_used = sem("v_used")
        gate_psum = sem("gate_psum")
        gate_sum = sem("gate_sum")
        gate_exp = sem("gate_exp")
        sig_ready = sem("sig_ready")
        sum_ready = sem("sum_ready")
        ms_psum = sem("ms_psum")
        ln_ready = sem("ln_ready")
        r_ready = sem("r_ready")
        qk_scaled = sem("qk_scaled")
        parts_ready = [sem(f"parts_ready{s}") for s in range(2)]
        ones_ready = sem("ones_ready")
        r_known = sem("r_known")
        r_rows_ready = sem("r_rows_ready")
        fill_ready = sem("fill_ready")
        fill_loaded = sem("fill_loaded")
        parts_stored = [sem(f"parts_stored{s}") for s in range(2)]
        m_stored = sem("m_stored")
        shift_rows_loaded = sem("shift_rows_loaded")
        ex_loaded = sem("ex_loaded")
        ex_scores = sem("ex_scores")
        ex_max = sem("ex_max")
        ex_mT = sem("ex_mT")
        ex_step = sem("ex_step")
        ex_parts = sem("ex_parts")
        ex_stored = sem("ex_stored")
        stack_loaded = [sem(f"stack_loaded{p}") for p in range(2)]
        v_staged = [sem(f"v_staged{p}") for p in range(2)]
        scores_ready = sem("scores_ready")
        probs_ready = sem("probs_ready")
        pv_done = sem("pv_done")
        acc_copied = sem("acc_copied")
        accT_psum = sem("accT_psum")
        norm_step = sem("norm_step")
        o_ready = sem("o_ready")
        o_psum = sem("o_psum")
        o_used = sem("o_used")
        out_ready = sem("out_ready")
        out_stored = sem("out_stored")

        x_dram = x.rearrange("b (t p) d -> p (b t) d", p=P)
        out_dram = out.rearrange("b (t p) d -> p (b t) d", p=P)

        def chunk(c):
            return slice(c * TC, (c + 1) * TC)

        def cols(c):
            return slice(c * 512, (c + 1) * 512)

        def h_bank(m):
            return ps[:, m % 2, :]

        def t_bank(n):
            return ps[:, (0 if n in (10, 11) else 2) + n % 2, :]

        def y_bank(f, c):
            return ps[:, 5 if c % 2 and not (f == 0 and c > 1) else 4, :]

        def o_bank(c):
            return ps[:, 5 - c % 2, :]

        V_BANK, Q_BANK, GATE_BANK = 5, 6, 0

        def per_head(w):
            return bass.AP(w.tensor, w.offset, [[0, 1], [0, H], [1, HD]])

        block = ctx.enter_context(nc.Block())

        @block.sync
        def _(sp):
            for c in range(C):
                sp.dma_start(x_in[:, chunk(c), :], x_dram[:, chunk(c), :]).then_inc(x_loaded[c], 16)
                if c == 0:
                    sp.dma_start(w1_sb[:], w1).then_inc(w1_loaded, 16)
            sp.dma_start(w2_sb[:], w2.rearrange("(m p) e -> p m e", p=P)).then_inc(w2_loaded, 16)
            sp.dma_start(b2_row[:], b2.partition_broadcast(P)).then_inc(rows_loaded, 16)
            sp.dma_start(qn_row[:], qn_w.partition_broadcast(P)).then_inc(r_w_loaded, 16)
            sp.dma_start(kn_row[:], kn_w.partition_broadcast(P)).then_inc(r_w_loaded, 16)
            sp.dma_start(wv_sb[:], Wv).then_inc(attn_w_loaded, 16)
            sp.dma_start(bv_row[:], bv.partition_broadcast(P)).then_inc(attn_w_loaded, 16)
            sp.dma_start(bg_row[:], bq[D:D + H].partition_broadcast(P)).then_inc(attn_w_loaded, 16)
            sp.dma_start(bo_row[:], bo.partition_broadcast(P)).then_inc(rows_loaded, 16)
            sp.dma_start(wo_sb[:], Wo).then_inc(wo_loaded, 16)

            def store_parts(s, b):
                for part in range(3):
                    sp.wait_ge(parts_ready[s], 3 * (2 * b + 1) + part + 1)
                    sp.dma_start(part_dram[s][b * GB:(b + 1) * GB, part], parts[:, s, part, :]
                                 ).then_inc(parts_stored[s], 16)

            sp.wait_ge(fill_ready, 1)
            sp.dma_start(m_dram.rearrange("g s (j n) -> (g s j) n", j=HG), m_zero[0:G * 3 * HG, :]).then_inc(m_stored, 16)
            for p in range(2):
                for st, rows, fill in ((q_st, slice(PROD, SH), m_zero), (k_st, slice(PROD, SH), m_zero),
                                       (k_st, slice(SH, ROWS), m_ones)):
                    n = rows.stop - rows.start
                    sp.dma_start(st[p][rows, :, :], fill[0:n, :].unsqueeze(1).to_broadcast([n, HG, N])
                                 ).then_inc(fill_loaded, 16)
            sp.wait_ge(r_rows_ready, 1)
            for p in range(2):
                for j in range(HG):
                    sp.dma_start(q_st[p][SH:SH + 3, j, :], r_rows[0:1, :, :]).then_inc(shift_rows_loaded, 16)
            sp.wait_ge(m_stored, 16)
            sp.wait_ge(fill_loaded, 16 * 2 * 3)
            sp.wait_ge(shift_rows_loaded, 16 * 2 * HG)

            def of_group(s, g):
                return part_dram[s].rearrange("g s (d j) t -> g (s d) (j t)", j=HG)[bass.ds(g, 1)]

            def load_q(g, p, done):
                q = of_group(0, g)
                for i in range(3):
                    rows = slice(3 * HD * i, 3 * HD * (i + 1))
                    qi = q[:, HD * i:HD * (i + 1), :]
                    qi = bass.AP(qi.tensor, qi.offset, [[0, 3], *qi.ap[1:]])
                    sp.dma_start(q_st[p][rows, :, :].rearrange("s j t -> s (j t)"), qi).then_inc(done, 16)
                sp.dma_start(q_st[p][SH + 3:SH + 6, :, :].rearrange("s j t -> s (j t)"),
                             m_dram[bass.ds(g, 1)].rearrange("g s n -> (g s) n")).then_inc(done, 16)

            def load_k(g, p, done):
                k = of_group(1, g)
                k = bass.AP(k.tensor, k.offset, [[0, 3], *k.ap[1:]])
                sp.dma_start(k_st[p][0:PROD, :, :].rearrange("s j t -> s (j t)"), k).then_inc(done, 16)

            sp.wait_ge(r_known, 1)
            large = sp.value_load(flag[0:1, 0:1], min_val=0, max_val=1)
            with sp.If(large > 0):
                for b in range(B):
                    for s in range(2):
                        store_parts(s, b)
                        sp.wait_ge(parts_stored[s], 16 * 3 * (b + 1))
                sp.sem_inc(ex_stored, 16)
                with sp.Fori(0, G) as g:
                    sp.wait_ge(ex_parts, g + 1)
                    load_q(g, 0, ex_loaded)
                    load_k(g, 0, ex_loaded)
                    sp.wait_ge(ex_parts, g + 2)
                    sp.dma_start(m_dram[bass.ds(g, 1)].rearrange("g s (u n) -> (g u) s n", u=HG * KT),
                                 mx_parts[:]).then_inc(ex_stored, 16)
                sp.wait_ge(ex_stored, 16 * (G + 1))
                for p in range(2):
                    load_q(p, p, stack_loaded[p])
                    load_k(p, p, stack_loaded[p])

            with sp.If(large < 1):
                store_parts(0, 0)
                store_parts(1, 0)
                sp.wait_ge(parts_stored[0], 16 * 3)
                load_q(0, 0, stack_loaded[0])
                sp.wait_ge(parts_stored[1], 16 * 3)
                load_k(0, 0, stack_loaded[0])
                load_q(1, 1, stack_loaded[1])
                load_k(1, 1, stack_loaded[1])
                for s in range(2):
                    store_parts(s, 1)
            for s in range(2):
                sp.wait_ge(parts_stored[s], 16 * 3 * B)
            with sp.Fori(1, PAIRS) as i:
                for p in range(2):
                    sp.wait_ge(scores_ready, (i - 1) * BT + (p + 1) * TILES)
                    load_q(i * 2 + p, p, stack_loaded[p])
                    load_k(i * 2 + p, p, stack_loaded[p])

            for c in range(C):
                sp.wait_ge(out_ready, c + 1)
                sp.dma_start(out_dram[:, chunk(c), :], y_out[:, chunk(c), :]).then_inc(out_stored, 16)
            sp.wait_ge(out_stored, 16 * C)

        @block.gpsimd
        def _(pool):
            nc.gpsimd.memset(ident[:], 0.0).then_inc(const_step, 1)
            nc.gpsimd.memset(minus_half[:], -0.5)
            nc.gpsimd.memset(eps[:], RMS_EPS).then_inc(const_step, 1)
            pool.wait_ge(const_step, 2)
            nc.gpsimd.affine_select(out=ident[:], in_=ident[:], compare_op=ALU.not_equal, fill=1.0, base=0,
                                    pattern=[[-1, P]], channel_multiplier=1).then_inc(consts_ready, 1)
            def inverse_std(stage, c):
                t = chunk(c)
                pool.wait_ge(stats_ready[stage], c + 1)
                nc.gpsimd.tensor_scalar(var_eps[:, t], mean_var[:, t, 1], LN_EPS, None, ALU.add).then_inc(var_ready, 1)
                pool.wait_ge(var_ready, stage * C + c + 1)
                nc.gpsimd.tensor_tensor(rstd[:, t], var_eps[:, t], minus_half[:, t], ALU.pow
                                        ).then_inc(rstd_ready[stage], 1)

            def scale_qk(c):
                for s in range(2):
                    pool.wait_ge(sum_ready, 2 * c + s + 1)
                    pool.wait_ge(r_ready, 2 * c + s + 1)
                    nc.gpsimd.tensor_tensor(qk[:, c, s, :], qk[:, c, s, :], qk_ms[:, c, s, :], ALU.mult
                                            ).then_inc(qk_scaled, 1)

            nc.gpsimd.memset(acc_sb[:, 1, :].bitcast(U32), ONES).then_inc(acc_copied, 1)
            nc.gpsimd.memset(acc_sb[:, 0, :].bitcast(U32), 0).then_inc(fill_ready, 1)
            nc.gpsimd.memset(v_aug[:], 1.0).then_inc(ones_ready, 1)
            for c in range(C):
                inverse_std(0, c)
            pool.wait_ge(rows_loaded, 32)
            nc.gpsimd.tensor_scalar(b2h_row[:], b2_row[:], 0.5, None, ALU.mult).then_inc(const_step, 1)
            pool.wait_ge(const_step, 3)
            for c in range(C):
                pool.wait_ge(x_loaded[c], 16)
                nc.gpsimd.tensor_tensor(x_b[:, chunk(c), :], x_in[:, chunk(c), :],
                                        b2h_row[:].unsqueeze(1).to_broadcast([P, TC, D]), ALU.add).then_inc(xb_ready, 1)
            def stage_v(i, p):
                nc.gpsimd.tensor_copy(v_st[p][:], v_aug[:, bass.ds(i * 2 + p, 1)].rearrange("p g k v -> p (g k) v")
                                      ).then_inc(v_staged[p], 1)

            for c in range(3):
                inverse_std(1, c)
            scale_qk(0)
            scale_qk(1)
            inverse_std(1, 3)
            pool.wait_ge(v_used, N // 512)
            for p in range(2):
                stage_v(0, p)
            scale_qk(2)
            scale_qk(3)
            pool.wait_ge(v_used, C)
            with pool.Fori(1, PAIRS) as i:
                for p in range(2):
                    pool.wait_ge(pv_done, (i - 1) * (2 * STEPS) + (p + 1) * STEPS + PB // 2)
                    stage_v(i, p)

            for c in range(C):
                nc.gpsimd.tensor_tensor(x_b[:, chunk(c), :], x_1[:, chunk(c), :],
                                        bo_row[:].unsqueeze(1).to_broadcast([P, TC, D]), ALU.add).then_inc(xb2_ready, 1)

            for c in range(C):
                inverse_std(2, c)
            for c in range(C):
                nc.gpsimd.tensor_tensor(x_b[:, chunk(c), :], x_2[:, chunk(c), :],
                                        b2h_row[:].unsqueeze(1).to_broadcast([P, TC, D]), ALU.add).then_inc(xb3_ready, 1)

        @block.scalar
        def _(act):
            act.dma_start(vec_rows[:], b1.rearrange("(m p) -> m p", p=P)).then_inc(vec_loaded, 16)
            nc.scalar.preload_act_table(ACT.Gelu)
            for row, vec in enumerate((bq[0:D], bk)):
                act.dma_start(qk_rows[row:row + 1, :], vec.unsqueeze(0)).then_inc(qk_rows_loaded, 16)
            for row, vec in ((2, qn_w), (3, kn_w)):
                act.dma_start(qk_rows[row:row + 1, :].rearrange("o (h d) -> o h d", d=HD), per_head(vec)
                              ).then_inc(qk_rows_loaded, 16)
            act.dma_start(wq_sb[:], Wq).then_inc(attn_w_loaded, 16)
            act.dma_start(wk_sb[:], Wk).then_inc(attn_w_loaded, 16)

            def copy_turned(n, dst, c):
                act.wait_ge(turned, n + 1)
                nc.scalar.copy(dst[:, cols(c)], t_bank(n)).then_inc(turned_copied, 1)

            def gelu(f, c, ms=range(M)):
                for m in ms:
                    act.wait_ge(h_psum[f], M * c + m + 1)
                    nc.scalar.activation(hT[:, c, m, :], h_bank(m), ACT.Gelu,
                                         bias=b1_col[:, m:m + 1]).then_inc(h_ready[f], 1)

            def qk_sums(c):
                for s, b_col in ((0, bq_col), (1, bk_col)):
                    act.wait_ge(qk_psum, 2 * c + s + 1)
                    if c >= 1:
                        act.wait_ge(ms_psum, 2 * c - 1 + s)
                    nc.scalar.activation(qk_sq[:, s, :], ps[:, Q_BANK + s, :], ACT.Square, bias=b_col)
                    nc.scalar.activation(qk[:, c, s, :], ps[:, Q_BANK + s, :], ACT.Identity,
                                         bias=qk_bw_col[:, s:s + 1], scale=qk_w_col[:, s:s + 1]).then_inc(sum_ready, 1)

            def inverse_rms(c):
                for s in range(2):
                    act.wait_ge(ms_psum, 2 * c + s + 1)
                    nc.scalar.activation(qk_ms[:, c, s, :], ps[:, Q_BANK + s, :], ACT.Ln, bias=eps[:, 0:1]
                                         ).then_inc(ln_ready, 1)
                for s in range(2):
                    act.wait_ge(ln_ready, 2 * c + s + 1)
                    nc.scalar.activation(qk_ms[:, c, s, :], qk_ms[:, c, s, :], ACT.Exp, scale=-0.5
                                         ).then_inc(r_ready, 1)

            copy_turned(0, x_nT, 0)
            act.wait_ge(vec_ready, 1)
            gelu(0, 0, (0, 1))
            copy_turned(1, x_nT, 1)
            gelu(0, 0, (2, 3))
            copy_turned(2, x_nT, 2)
            gelu(0, 1)
            copy_turned(3, x_nT, 3)
            gelu(0, 2)
            gelu(0, 3)
            act.wait_ge(consts_ready, 1)
            nc.scalar.preload_act_table_set("natural_log_exp_and_others")
            copy_turned(4, x_nT, 0)
            act.wait_ge(vec_ready, 3)
            qk_sums(0)
            copy_turned(5, x_nT, 1)
            inverse_rms(0)
            qk_sums(1)
            copy_turned(6, x_nT, 2)
            inverse_rms(1)
            qk_sums(2)
            copy_turned(7, x_nT, 3)
            inverse_rms(2)
            qk_sums(3)
            inverse_rms(3)
            act.wait_ge(gate_sum, 1)
            nc.scalar.activation(gate[:], gate[:], ACT.Exp, scale=-1.0).then_inc(gate_exp, 1)

            act.wait_ge(v_used, C)
            act.wait_ge(gate_sum, 1)
            act.sem_inc(probs_ready, FREE3)

            def exp_tiles(i, first, last):
                for n in range(first, last):
                    act.wait_ge(scores_ready, i * BT + n + 1)
                    act.wait_ge(pv_done, i * (BT // 2) + n // 2 + 1)
                    b = SBUF_OF[n]
                    nc.scalar.activation(probs[:, n % PB, :], ps[:, 2 * b:2 * b + 2, :].rearrange("p b n -> p (b n)"),
                                         ACT.Exp).then_inc(probs_ready, 1)

            with act.Fori(0, PAIRS) as i:
                exp_tiles(i, 0, BT)

            for c in range(C):
                copy_turned(8 + c, oT, c)
            nc.scalar.preload_act_table(ACT.Gelu)
            copy_turned(12, x_nT, 0)
            gelu(1, 0, (0, 1, 2))
            copy_turned(13, x_nT, 1)
            gelu(1, 0, (3,))
            gelu(1, 1)
            copy_turned(14, x_nT, 2)
            copy_turned(15, x_nT, 3)
            gelu(1, 2)
            gelu(1, 3)

        @block.vector
        def _(dve):
            count = [0]

            def done(ins):
                count[0] += 1
                ins.then_inc(dve_step, 1)
                dve.wait_ge(dve_step, count[0])

            def token_stats(stage, src, c):
                for t in range(c * TC, (c + 1) * TC):
                    last = nc.vector.bn_stats(stats[:, t, :], src[:, t, :])
                done(last)
                for t in range(c * TC, (c + 1) * TC):
                    last = nc.vector.bn_aggr(mean_var[:, t, :], stats[:, t, :])
                last.then_inc(stats_ready[stage], 1)

            def normalise(stage, src, c):
                dve.wait_ge(rstd_ready[stage], c + 1)
                dve.wait_ge(stats_ready[stage], c + 1)
                for t in range(c * TC, (c + 1) * TC):
                    last = nc.vector.tensor_scalar(x_n[:, t, :], src[:, t, :], mean_var[:, t, 0:1], rstd[:, t:t + 1],
                                                   ALU.subtract, ALU.mult)
                last.then_inc(xn_ready[stage], 1)

            dve.sem_inc(o_ready, FREE2)
            for c in range(C):
                if c == 3:
                    dve.wait_ge(vec_psum, 1)
                    nc.vector.tensor_copy(vec_cols[:, 0:M], ps[:, 7, 0:M]).then_inc(vec_ready, 1)
                dve.wait_ge(x_loaded[c], 16)
                token_stats(0, x_in, c)
                if c >= 1:
                    normalise(0, x_in, c - 1)
            normalise(0, x_in, C - 1)

            dve.wait_ge(qk_rows_loaded, 16 * 4)
            nc.vector.tensor_copy(qk_rows_p[:].rearrange("p (g d j) -> p g d j", d=HD, j=HG),
                                  qk_rows[:].rearrange("p (g j d) -> p g d j", d=HD, j=HG)).then_inc(qk_rows_ready, 1)
            dve.wait_ge(attn_w_loaded, 16 * 5)
            for s, w in ((0, wq_sb[:, 0:D]), (1, wk_sb[:])):
                last = nc.vector.tensor_copy(wqk_p[:, s, :].rearrange("p (g d j) -> p g d j", d=HD, j=HG),
                                             w.rearrange("p (g j d) -> p g d j", d=HD, j=HG))
            last.then_inc(qk_w_ready, 1)
            dve.wait_ge(consts_ready, 1)
            done(nc.vector.reduce_sum(head_sum[:].rearrange("p (g j) -> p g j", j=HG),
                                      ident[:].rearrange("p (g d j) -> p g j d", d=HD, j=HG), AX_X))
            nc.vector.tensor_scalar(head_mean[:].rearrange("p (g d j) -> p g d j", d=HD, j=HG),
                                    head_sum[:].rearrange("p (g j) -> p g j", j=HG).unsqueeze(2)
                                    .to_broadcast([P, GB, HD, HG]), 1.0 / HD, None, ALU.mult).then_inc(consts_ready, 1)
            dve.wait_ge(vec_psum, 2)
            nc.vector.tensor_copy(vec_cols[:, M:M + 4], ps[:, 7, M:M + 4]).then_inc(vec_ready, 1)
            dve.wait_ge(vec_ready, 2)
            nc.vector.tensor_copy(qk_w_col[:, 1:2], kn_col)
            done(nc.vector.tensor_scalar(qk_w_col[:, 0:1], qn_col, float(HD) ** -0.5, None, ALU.mult))
            nc.vector.tensor_tensor(qk_bw_col[:], vec_cols[:, M:M + 2], qk_w_col[:], ALU.mult).then_inc(vec_ready, 1)
            dve.wait_ge(r_w_loaded, 16 * 2)
            done(nc.vector.tensor_tensor(r_w[:, 0, :], qn_row[:], kn_row[:], ALU.mult))
            done(nc.vector.tensor_scalar(r_w[:, 1, :], r_w[:, 0, :], -1.0, None, ALU.mult))
            done(nc.vector.tensor_tensor(r_w[:, 2, :], r_w[:, 0, :], r_w[:, 1, :], ALU.max))
            done(nc.vector.reduce_max(r_col[:, 0:1], r_w[:, 2, :], AX_X))
            done(nc.vector.tensor_scalar(r_col[:, 1:2], r_col[:, 0:1], -float(HD) ** 0.5, None, ALU.mult))
            nc.vector.tensor_scalar(flag[:], r_col[:, 1:2], -SHIFT_SAFE, None, ALU.is_lt).then_inc(r_known, 1)
            done(nc.vector.tensor_copy(r_bf[:, 0:1], r_col[:, 1:2]))
            done(nc.vector.tensor_tensor(r_col[:, 2:3], r_col[:, 1:2], r_bf[:, 0:1], ALU.subtract))
            done(nc.vector.tensor_copy(r_bf[:, 1:2], r_col[:, 2:3]))
            done(nc.vector.tensor_tensor(r_col[:, 3:4], r_col[:, 2:3], r_bf[:, 1:2], ALU.subtract))
            for s, part in enumerate((r_bf[0:1, 0:1], r_bf[0:1, 1:2], r_col[0:1, 3:4])):
                last = nc.vector.tensor_copy(r_rows[0:1, s, :], part.to_broadcast([1, N]))
            last.then_inc(r_rows_ready, 1)

            def ffn_sum(c):
                dve.wait_ge(xb_ready, c + 1)
                dve.wait_ge(y_psum[0], c + 1)
                ins = nc.vector.scalar_tensor_tensor(
                    out=x_1[:, chunk(c), :].rearrange("p t d -> p (t d)"), in0=y_bank(0, c), scalar=0.5,
                    in1=x_b[:, chunk(c), :].rearrange("p t d -> p (t d)"), op0=ALU.mult, op1=ALU.add)
                ins.then_inc(y_used[0], 1)
                dve.wait_ge(y_used[0], c + 1)
                token_stats(1, x_1, c)

            def v_sum(c):
                dve.wait_ge(v_psum, c + 1)
                for tl in range(TC):
                    b, kt = divmod(c * TC + tl, KT)
                    last = nc.vector.tensor_tensor(
                        v_aug[:, b * GB:(b + 1) * GB, kt, :].rearrange("p g (j v) -> p g j v", v=VW)[:, :, :, 0:HD],
                        ps[:, V_BANK, tl * D:(tl + 1) * D].rearrange("p (g j d) -> p g j d", j=HG, d=HD),
                        bv_row[:].rearrange("p (g j d) -> p g j d", j=HG, d=HD), ALU.add)
                last.then_inc(v_used, 1)

            def split(s, c):
                b = c * 512 // N
                if b > 0:
                    dve.wait_ge(parts_stored[s], 16 * 3 * b)
                at = slice(c * 512 % N, c * 512 % N + 512)
                dve.wait_ge(qk_scaled, 2 * c + s + 1)
                x = qk[:, c, s, :]
                nc.vector.tensor_copy(parts[:, s, 0, at], x).then_inc(parts_ready[s], 1)
                dve.wait_ge(parts_ready[s], 3 * c + 1)
                done(nc.vector.tensor_tensor(x, x, parts[:, s, 0, at], ALU.subtract))
                nc.vector.tensor_copy(parts[:, s, 1, at], x).then_inc(parts_ready[s], 1)
                dve.wait_ge(parts_ready[s], 3 * c + 2)
                nc.vector.tensor_tensor(parts[:, s, 2, at], x, parts[:, s, 1, at],
                                        ALU.subtract).then_inc(parts_ready[s], 1)

            ffn_sum(0)
            normalise(1, x_1, 0)
            ffn_sum(1)
            normalise(1, x_1, 1)
            dve.wait_ge(attn_w_loaded, 16 * 5)
            dve.wait_ge(ones_ready, 1)
            ffn_sum(2)
            v_sum(0)
            normalise(1, x_1, 2)
            split(0, 0)
            v_sum(1)
            split(1, 0)
            ffn_sum(3)
            split(0, 1)
            normalise(1, x_1, 3)
            split(1, 1)
            v_sum(2)
            v_sum(3)
            dve.wait_ge(gate_psum, 2)
            nc.vector.tensor_tensor(gate[:], ps[:, GATE_BANK, 0:T * H].rearrange("p (t h) -> p t h", h=H),
                                    bg_row[:].unsqueeze(1).to_broadcast([P, T, H]), ALU.add).then_inc(gate_sum, 1)
            split(0, 2)
            split(0, 3)
            split(1, 2)
            split(1, 3)
            dve.wait_ge(gate_exp, 1)
            done(nc.vector.tensor_scalar(gate[:], gate[:], 1.0, None, ALU.add))
            for b in range(B):
                last = nc.vector.reciprocal(
                    sig[:, b * GB:(b + 1) * GB, :, :],
                    gate[:, b * KT:(b + 1) * KT, :].rearrange("p t (g j) -> p g t j", j=HG))
            last.then_inc(sig_ready, 1)

            dve.wait_ge(r_known, 1)
            large = dve.value_load(flag[0:1, 0:1], min_val=0, max_val=1)
            U = HG * KT
            with dve.If(large > 0):
                dve.sem_inc(ex_parts, 1)
                with dve.Fori(0, G) as g:
                    for u in range(U):
                        dve.wait_ge(ex_scores, g * U + u + 1)
                        nc.vector.reduce_max(mx[:, u:u + 1], ps[:, 2 * (u % 2):2 * (u % 2) + 2, :]
                                             .rearrange("p b n -> p (b n)"), AX_X).then_inc(ex_max, 1)
                    dve.wait_ge(ex_mT, g + 1)
                    nc.vector.tensor_scalar(mx_n[:], ps[0:U, 4, 0:P], -1.0, None, ALU.mult).then_inc(ex_step, 1)
                    dve.wait_ge(ex_step, g * 4 + 1)
                    dve.wait_ge(ex_stored, g * 16 + 16)
                    nc.vector.tensor_copy(mx_parts[:, 0, :], mx_n[:]).then_inc(ex_step, 1)
                    dve.wait_ge(ex_step, g * 4 + 2)
                    nc.vector.tensor_tensor(mx_r[:], mx_n[:], mx_parts[:, 0, :], ALU.subtract).then_inc(ex_step, 1)
                    dve.wait_ge(ex_step, g * 4 + 3)
                    nc.vector.tensor_copy(mx_parts[:, 1, :], mx_r[:]).then_inc(ex_step, 1)
                    dve.wait_ge(ex_step, g * 4 + 4)
                    nc.vector.tensor_tensor(mx_parts[:, 2, :], mx_r[:], mx_parts[:, 1, :],
                                            ALU.subtract).then_inc(ex_parts, 1)

            dve.wait_ge(sig_ready, 1)
            def item(b, i, k):
                return (b * (GB // 2) + i) * 4 + k

            def save_sums(b, i, k):
                dve.wait_ge(pv_done, item(b, i, k) * KT + KT + PB // 2)
                nc.vector.tensor_copy(acc_sb[:, k % 2, :], ps[:, ACC + k % 2, :]).then_inc(acc_copied, 1)

            def divide(b, i, k):
                half = k % 2
                g = b * GB + i * 2 + k // 2
                heads = bass.ds((i * 2 + k // 2) * (HG * HD), HG * HD)
                dve.wait_ge(accT_psum, (item(b, i, k) + 1) * 4 + 4)
                rows = ps[:, ACC + half, :].rearrange("p (t j v) -> p t j v", j=HG, v=32)
                nc.vector.reciprocal(r_den[:], rows[:, :, :, HD]).then_inc(norm_step, 1)
                dve.wait_ge(norm_step, item(b, i, k) * 2 + 1)
                nc.vector.tensor_tensor(fac[:], r_den[:], sig[:, bass.ds(g, 1), 4 * half:4 * half + 4, :]
                                        .rearrange("p g t j -> p (g t) j"), ALU.mult).then_inc(norm_step, 1)
                dve.wait_ge(norm_step, item(b, i, k) * 2 + 2)
                nc.vector.tensor_tensor(
                    o_nat[:, bass.ds(b * KT + 4 * half, 4), heads].rearrange("p t (j d) -> p t j d", d=HD),
                    rows[:, :, :, 0:HD], fac[:].unsqueeze(3).to_broadcast([P, 4, HG, HD]),
                    ALU.mult).then_inc(o_ready, 1)

            def finish(b, i, items):
                for k in items:
                    save_sums(b, i, k)
                    divide(b, i, k)

            with dve.Fori(0, B - 1) as b:
                with dve.Fori(0, GB // 2) as i:
                    finish(b, i, range(4))
            with dve.Fori(0, GB // 2 - 1) as i:
                finish(B - 1, i, range(4))
            finish(B - 1, GB // 2 - 1, range(3))
            save_sums(B - 1, GB // 2 - 1, 3)

            def o_sum(c):
                dve.wait_ge(xb2_ready, c + 1)
                dve.wait_ge(o_psum, c + 1)
                nc.vector.tensor_tensor(x_2[:, chunk(c), :].rearrange("p t d -> p (t d)"), o_bank(c),
                                        x_b[:, chunk(c), :].rearrange("p t d -> p (t d)"), ALU.add).then_inc(o_used, 1)
                dve.wait_ge(o_used, c + 1)
                token_stats(2, x_2, c)

            o_sum(0)
            divide(B - 1, GB // 2 - 1, 3)
            normalise(2, x_2, 0)
            o_sum(1)
            normalise(2, x_2, 1)
            o_sum(2)
            o_sum(3)
            normalise(2, x_2, 2)
            normalise(2, x_2, 3)
            for c in range(C):
                dve.wait_ge(xb3_ready, c + 1)
                dve.wait_ge(y_psum[1], c + 1)
                nc.vector.scalar_tensor_tensor(
                    out=y_out[:, chunk(c), :].rearrange("p t d -> p (t d)"), in0=y_bank(1, c), scalar=0.5,
                    in1=x_b[:, chunk(c), :].rearrange("p t d -> p (t d)"), op0=ALU.mult, op1=ALU.add
                ).then_inc(out_ready, 1)

        @block.tensor
        def _(pe):
            def turn_chunk(n, src, c):
                if 2 <= n < 8 or n >= 14:
                    pe.wait_ge(turned_copied, n - 1)
                elif n >= 12:
                    pe.wait_ge(turned_copied, n - 3)
                for tl in range(TC):
                    last = nc.tensor.transpose(t_bank(n)[:, tl * P:(tl + 1) * P], src[:, c * TC + tl, :], ident[:])
                last.then_inc(turned, 1)

            def turn_xn(n, stage, c):
                pe.wait_ge(xn_ready[stage], c + 1)
                turn_chunk(n, x_n, c)

            def ffn_in(f, n, c, ms=range(M)):
                pe.wait_ge(turned_copied, n + 1)
                for m in ms:
                    if M * c + m >= 2:
                        pe.wait_ge(h_ready[f], M * c + m - 1)
                    nc.tensor.matmul(h_bank(m), w1_sb[:, m * P:(m + 1) * P], x_nT[:, cols(c)],
                                     start=True, stop=True).then_inc(h_psum[f], 1)

            def ffn_out(f, c, used, tls=range(TC)):
                pe.wait_ge(h_ready[f], M * (c + 1))
                if c >= 2:
                    pe.wait_ge(used, c if (f, c) == (0, 3) else c - 1)
                for tl in tls:
                    for m in range(M):
                        last = nc.tensor.matmul(y_bank(f, c)[:, tl * D:(tl + 1) * D], hT[:, c, m, tl * P:(tl + 1) * P],
                                                w2_sb[:, m, :], start=(m == 0), stop=(m == M - 1))
                if tl == TC - 1:
                    last.then_inc(y_psum[f], 1)

            def qkv(n, c):
                pe.wait_ge(turned_copied, n + 1)
                for s, w in ((0, wqk_p[:, 0, :]), (1, wqk_p[:, 1, :])):
                    if c >= 1:
                        pe.wait_ge(ln_ready, 2 * c - 1 + s)
                    nc.tensor.matmul(ps[:, Q_BANK + s, :], w, x_nT[:, cols(c)], start=True, stop=True
                                     ).then_inc(qk_psum, 1)
                if c == 0:
                    pe.wait_ge(y_used[0], 2)
                else:
                    pe.wait_ge(v_used, c)
                for tl in range(TC):
                    t = c * TC + tl
                    last = nc.tensor.matmul(ps[:, V_BANK, tl * D:(tl + 1) * D], x_nT[:, t * P:(t + 1) * P], wv_sb[:],
                                            start=True, stop=True)
                last.then_inc(v_psum, 1)

            def mean_squares(c):
                for s in range(2):
                    pe.wait_ge(sum_ready, 2 * c + s + 1)
                    nc.tensor.matmul(ps[:, Q_BANK + s, :], head_mean[:], qk_sq[:, s, :], start=True, stop=True
                                     ).then_inc(ms_psum, 1)

            def gates(first, last):
                for t in range(first, last):
                    ins = nc.tensor.matmul(ps[:, GATE_BANK, t * H:(t + 1) * H], x_nT[:, t * P:(t + 1) * P],
                                           wq_sb[:, D:D + H], start=True, stop=True)
                ins.then_inc(gate_psum, 1)

            pe.wait_ge(consts_ready, 1)
            turn_xn(0, 0, 0)
            pe.wait_ge(vec_loaded, 16)
            nc.tensor.transpose(ps[:, 7, 0:M], vec_rows[:], ident[0:M, 0:M]).then_inc(vec_psum, 1)
            pe.wait_ge(w1_loaded, 16)
            ffn_in(0, 0, 0, (0, 1))
            turn_xn(1, 0, 1)
            ffn_in(0, 0, 0, (2, 3))
            turn_xn(2, 0, 2)
            pe.wait_ge(qk_rows_ready, 1)
            pe.wait_ge(vec_ready, 1)
            nc.tensor.transpose(ps[:, 7, M:M + 4], qk_rows_p[:], ident[0:4, 0:4]).then_inc(vec_psum, 1)
            ffn_in(0, 1, 1)
            turn_xn(3, 0, 3)
            ffn_in(0, 2, 2)
            pe.wait_ge(w2_loaded, 16)
            ffn_out(0, 0, y_used[0])
            ffn_in(0, 3, 3)
            ffn_out(0, 1, y_used[0])
            turn_xn(4, 1, 0)
            ffn_out(0, 2, y_used[0])
            pe.wait_ge(attn_w_loaded, 16 * 5)
            pe.wait_ge(qk_w_ready, 1)
            qkv(4, 0)
            turn_xn(5, 1, 1)
            pe.wait_ge(consts_ready, 2)
            mean_squares(0)
            qkv(5, 1)
            turn_xn(6, 1, 2)
            ffn_out(0, 3, y_used[0], (0, 1))
            mean_squares(1)
            ffn_out(0, 3, y_used[0], (2, 3))
            qkv(6, 2)
            pe.wait_ge(h_ready[0], M * C)
            gates(0, 12)
            turn_xn(7, 1, 3)
            mean_squares(2)
            qkv(7, 3)
            gates(12, T)
            mean_squares(3)

            pe.wait_ge(y_used[0], C)
            pe.wait_ge(v_used, C)
            pe.wait_ge(turned_copied, 2 * C)
            pe.wait_ge(ln_ready, 2 * C)
            pe.wait_ge(gate_sum, 1)

            pe.wait_ge(r_known, 1)
            large = pe.value_load(flag[0:1, 0:1], min_val=0, max_val=1)
            U = HG * KT
            with pe.If(large > 0):
                pe.sem_inc(ex_max, 2)
                with pe.Fori(0, G) as g:
                    pe.wait_ge(ex_loaded, g * (16 * LOADS) + 16 * LOADS)
                    for u in range(U):
                        j, qt = divmod(u, KT)
                        pe.wait_ge(ex_max, g * U + u + 1)
                        for h in range(2):
                            last = nc.tensor.matmul(ps[:, 2 * (u % 2) + h, :], q_st[0][0:ROWS, j, qt * P:(qt + 1) * P],
                                                    k_st[0][0:ROWS, j, h * 512:(h + 1) * 512], start=True, stop=True)
                        last.then_inc(ex_scores, 1)
                    pe.wait_ge(ex_max, g * U + U + 2)
                    nc.tensor.transpose(ps[0:U, 4, 0:P], mx[:], ident[:]).then_inc(ex_mT, 1)
                pe.wait_ge(ex_parts, G + 1)

            pe.sem_inc(pv_done, PB // 2)

            def scores(i, n, wait=True):
                p, m = divmod(n % BT, TILES)
                step, jj = divmod(m, 2)
                half, kt = divmod(step, KT)
                if m == 0:
                    pe.wait_ge(stack_loaded[p], (i + n // BT) * (16 * LOADS) + 16 * LOADS)
                pe.wait_ge(probs_ready, i * BT + (n - n % BT) + PREV[n % BT] + 1 + FREE3)
                for u in range(2):
                    j = 2 * jj + u
                    last = nc.tensor.matmul(ps[:, 2 * SBUF_OF[n % BT] + u, :],
                                            k_st[p][0:ROWS, j, kt * P:(kt + 1) * P],
                                            q_st[p][0:ROWS, j, half * 512:(half + 1) * 512], start=True, stop=True)
                last.then_inc(scores_ready, 1)

            def weighted(i, s):
                p, step = divmod(s, STEPS)
                half, kt = divmod(step, KT)
                if step == 0:
                    pe.wait_ge(v_staged[p], i + 1)
                if kt == 0:
                    pe.wait_ge(o_ready, i * 4 + 2 * p + half + 1)
                pe.wait_ge(probs_ready, i * BT + 2 * s + 2 + FREE3)
                for j in range(HG):
                    last = nc.tensor.matmul(ps[32 * j:32 * j + VW, ACC + half, :],
                                            v_st[p][:, kt, j * VW:(j + 1) * VW],
                                            probs[:, (2 * s + j // 2) % PB, (j % 2) * 512:(j % 2 + 1) * 512],
                                            start=(kt == 0), stop=(kt == KT - 1))
                last.then_inc(pv_done, 1)

            def turn(i, k, t):
                half = k % 2
                pe.wait_ge(acc_copied, i * 4 + k + 2)
                nc.tensor.transpose(ps[:, ACC + half, t * P:(t + 1) * P],
                                    acc_sb[:, half, t * P:(t + 1) * P], ident[:]).then_inc(accT_psum, 1)

            def turn_o(n, c):
                pe.wait_ge(o_ready, FREE2 + (c * 512 // N + 1) * 2 * GB - 1 + c % 2)
                turn_chunk(n, o_nat, c)

            def iteration(i, final):
                for s in range(2 * STEPS):
                    if final and s == 2 * STEPS - 1:
                        turn_o(8, 0)
                        turn_o(9, 1)
                    if not (final and 2 * s + 4 >= BT):
                        scores(i, 2 * s + 4)
                    weighted(i, s)
                    if not (final and 2 * s + 5 >= BT):
                        scores(i, 2 * s + 5)
                    if 1 <= s % KT <= 4:
                        turn(i, s // KT - 1, s % KT - 1)

            for n in range(4):
                scores(0, n)
            with pe.Fori(0, PAIRS - 1) as i:
                iteration(i, False)
            iteration(PAIRS - 1, True)

            pe.wait_ge(wo_loaded, 16)
            def project(c):
                pe.wait_ge(turned_copied, 2 * C + c + 1)
                if c >= 2:
                    pe.wait_ge(o_used, c - 1)
                for tl in range(TC):
                    t = c * TC + tl
                    last = nc.tensor.matmul(o_bank(c)[:, tl * D:(tl + 1) * D], oT[:, t * P:(t + 1) * P], wo_sb[:],
                                            start=True, stop=True)
                last.then_inc(o_psum, 1)

            project(0)
            for t in range(4):
                turn(PAIRS - 1, 3, t)
            turn_o(10, 2)
            project(1)
            project(2)
            turn_o(11, 3)
            turn_xn(12, 2, 0)
            project(3)
            ffn_in(1, 12, 0, (0, 1, 2))
            turn_xn(13, 2, 1)
            ffn_in(1, 12, 0, (3,))
            ffn_in(1, 13, 1)
            turn_xn(14, 2, 2)
            pe.wait_ge(o_used, C)
            ffn_out(1, 0, out_ready)
            turn_xn(15, 2, 3)
            ffn_in(1, 14, 2)
            ffn_in(1, 15, 3)
            ffn_out(1, 1, out_ready)
            ffn_out(1, 2, out_ready)
            ffn_out(1, 3, out_ready)


_INS = ["L0_attn_x", "L0_attn_Wq", "L0_attn_bq", "L0_attn_Wk", "L0_attn_bk", "L0_attn_Wv", "L0_attn_bv",
        "L0_attn_Wo", "L0_attn_bo", "L0_attn_qn_w", "L0_attn_kn_w", "L0_ffn_w1", "L0_ffn_b1", "L0_ffn_w2",
        "L0_ffn_b2"]
_OUTS = [((2, 1024, 128), "float32")]


def kernel(**inputs):
    import numpy as _np
    import concourse.bacc as _bacc
    from concourse import mybir as _mybir
    from concourse.bass_utils import run_bass_kernel_spmd as _run

    nc = _bacc.Bacc("TRN2", target_bir_lowering=False, num_devices=1)
    arrays, args = {}, []
    for name in _INS:
        a = _np.ascontiguousarray(inputs[name])
        arrays[f"in_{name}"] = a
        args.append(nc.dram_tensor(f"in_{name}", a.shape, _mybir.dt.from_np(a.dtype), kind="ExternalInput").ap())
    for i, (shape, dtype) in enumerate(_OUTS):
        dt = _mybir.dt.from_np(_np.dtype(dtype))
        args.append(nc.dram_tensor(f"out_{i}", shape, dt, kind="ExternalOutput").ap())
    macaron_kernel(nc, *args)
    r = _run(nc, [arrays], core_ids=[0])
    got = tuple(r.results[0][f"out_{i}"] for i in range(len(_OUTS)))
    return got[0]
```
